# Optimizing a Trainium2 kernel written in Bass

```python
import numpy as np
import jax
import jax.numpy as jnp

def _softmax(x, axis=-1):
    return jax.nn.softmax(x, axis=axis)

def _gelu(x):
    return jax.nn.gelu(x, approximate=True)

def _silu(x):
    return jax.nn.silu(x)

def _sigmoid(x):
    return jax.nn.sigmoid(x)

def _layernorm(x, axis=-1, eps=1e-05):
    m = jnp.mean(x, axis=axis, keepdims=True)
    v = jnp.var(x, axis=axis, keepdims=True)
    return (x - m) / jnp.sqrt(v + eps)

def _scatter_add(tgt, idx, src, axis=0):
    return tgt.at[idx].add(src)

def _segment_sum(src, seg, n):
    return jax.ops.segment_sum(src, seg, n)
kernel_name = 'mk_decoder_postln_d1_seqx_r8_b8b485'

def setup_inputs(seed: int=0):
    np.random.seed(seed)
    _w = jnp.asarray

    def _rec_inputs():
        import jax
        import jax.numpy as jnp
        _rk = jax.random.key(seed)
        x = -0.000929 + 1 * jax.random.normal(jax.random.fold_in(_rk, 1), (4, 256, 128), jnp.float32)
        _lenS = 256 - jax.random.randint(jax.random.fold_in(_rk, 7), (4,), 0, max(1, 256 // 4) + 1, jnp.int32)
        _lenS2 = 512 - jax.random.randint(jax.random.fold_in(_rk, 8), (4,), 0, max(1, 512 // 4) + 1, jnp.int32)
        _ctx_1024P = jax.random.normal(jax.random.fold_in(_rk, 11), (4, 16, 128), jnp.float32)
        _ctx_1024c = jax.random.dirichlet(jax.random.fold_in(_rk, 511), 0.3 * jnp.ones((16,), jnp.float32), (4, 512))
        _ctx_1024t = jnp.einsum('bsk,bkd->bsd', _ctx_1024c, _ctx_1024P)
        _ctx_1024t = _ctx_1024t * jax.lax.rsqrt(jnp.mean(jnp.square(_ctx_1024t)) + 1e-12) * 0.953939
        ctx_1024 = -1.52775e-05 + 0.999936 * (_ctx_1024t + 0.3 * jax.random.normal(jax.random.fold_in(_rk, 611), (4, 512, 128), jnp.float32))
        return (x, ctx_1024)
    x, ctx_1024 = _rec_inputs()

    def _L0_attn_setup():
        import jax, jax.numpy as jnp
        import numpy as np
        N_HEADS = 16
        key = jax.random.key(seed)
        k_x, k_q, k_k, k_v, k_o = jax.random.split(key, 5)
        N, S, D = (8, 512, 128)
        scale = 0.02
        return {'x': jax.random.normal(k_x, (N, S, D), dtype=jnp.float32), 'Wq': jax.random.normal(k_q, (D, D), dtype=jnp.float32) * scale, 'Wk': jax.random.normal(k_k, (D, D), dtype=jnp.float32) * scale, 'Wv': jax.random.normal(k_v, (D, D), dtype=jnp.float32) * scale, 'Wo': jax.random.normal(k_o, (D, D), dtype=jnp.float32) * scale, 'bo': jnp.zeros((D,), dtype=jnp.float32)}
    _L0_attn_all = _L0_attn_setup()
    _L0_attn_in = {k: v for k, v in _L0_attn_all.items() if k in ('Wq', 'Wk', 'Wv', 'Wo', 'bo')}
    del _L0_attn_all

    def _L0_xattn_setup():
        import jax, jax.numpy as jnp
        import numpy as np
        B, N, L, D, H = (8, 128, 512, 128, 16)
        key = jax.random.key(seed)
        ks = jax.random.split(key, 7)
        s = 1.0 / np.sqrt(D)
        return {'q': jax.random.normal(ks[0], (B, N, D), dtype=jnp.float32), 'k': jax.random.normal(ks[1], (B, L, D), dtype=jnp.float32), 'v': jax.random.normal(ks[2], (B, L, D), dtype=jnp.float32), 'Wq': jax.random.normal(ks[3], (D, D), dtype=jnp.float32) * s, 'Wk': jax.random.normal(ks[4], (D, D), dtype=jnp.float32) * s, 'Wv': jax.random.normal(ks[5], (D, D), dtype=jnp.float32) * s, 'Wo': jax.random.normal(ks[6], (D, D), dtype=jnp.float32) * s}
    _L0_xattn_all = _L0_xattn_setup()
    _L0_xattn_in = {k: v for k, v in _L0_xattn_all.items() if k in ('Wq', 'Wk', 'Wv', 'Wo')}
    del _L0_xattn_all

    def _L0_ffn_setup():
        import jax, jax.numpy as jnp
        import numpy as np
        import math
        N_EXP = 8
        TOP_K = 2
        CAPACITY_FACTOR = 1.25

        def _capacity(num_tokens):
            cap = math.floor(TOP_K * CAPACITY_FACTOR * num_tokens / N_EXP)
            cap += cap % 2
            return int(cap)
        key = jax.random.key(seed)
        k1, k2, k3, k4 = jax.random.split(key, 4)
        B, C, d = (4, 128, 128)
        x = jax.random.normal(k1, (B, C, d), dtype=jnp.float32)
        w_g = jax.random.normal(k2, (d, N_EXP), dtype=jnp.float32) * 0.02
        c_fc = jax.random.normal(k3, (N_EXP, d, 4 * d), dtype=jnp.float32) * 0.02
        c_proj = jax.random.normal(k4, (N_EXP, 4 * d, d), dtype=jnp.float32) * 0.02
        return {'x': x, 'w_g': w_g, 'c_fc': c_fc, 'c_proj': c_proj}
    _L0_ffn_all = _L0_ffn_setup()
    _L0_ffn_in = {k: v for k, v in _L0_ffn_all.items() if k in ('w_g', 'c_fc', 'c_proj')}
    del _L0_ffn_all
    return {'x': x, 'ctx_1024': ctx_1024, 'L0_attn_Wq': _L0_attn_in['Wq'], 'L0_attn_Wk': _L0_attn_in['Wk'], 'L0_attn_Wv': _L0_attn_in['Wv'], 'L0_attn_Wo': _L0_attn_in['Wo'], 'L0_attn_bo': _L0_attn_in['bo'], 'L0_xattn_Wq': _L0_xattn_in['Wq'], 'L0_xattn_Wk': _L0_xattn_in['Wk'], 'L0_xattn_Wv': _L0_xattn_in['Wv'], 'L0_xattn_Wo': _L0_xattn_in['Wo'], 'L0_ffn_w_g': _L0_ffn_in['w_g'], 'L0_ffn_c_fc': _L0_ffn_in['c_fc'], 'L0_ffn_c_proj': _L0_ffn_in['c_proj']}

def reference(x, ctx_1024, L0_attn_Wq, L0_attn_Wk, L0_attn_Wv, L0_attn_Wo, L0_attn_bo, L0_xattn_Wq, L0_xattn_Wk, L0_xattn_Wv, L0_xattn_Wo, L0_ffn_w_g, L0_ffn_c_fc, L0_ffn_c_proj):
    import jax
    import jax.numpy as jnp

    def _L0_attn_ref(x, Wq, Wk, Wv, Wo, bo):
        import jax, jax.numpy as jnp
        import numpy as np
        N_HEADS = 16
        N, S, D = x.shape
        H = N_HEADS
        hd = D // H
        q = (x @ Wq.T).reshape(N, S, H, hd).transpose(0, 2, 1, 3)
        k = (x @ Wk.T).reshape(N, S, H, hd).transpose(0, 2, 1, 3)
        v = (x @ Wv.T).reshape(N, S, H, hd).transpose(0, 2, 1, 3)
        att = jnp.einsum('nqhd,nkhd->nhqk', q, k)
        att = jax.nn.softmax(att / jnp.sqrt(jnp.asarray(hd, x.dtype)), axis=3)
        out = jnp.einsum('nhqk,nkhd->nqhd', att, v).reshape(N, S, D)
        return out @ Wo.T + bo

    def _L0_xattn_ref(q, k, v, Wq, Wk, Wv, Wo):
        import jax, jax.numpy as jnp
        import numpy as np
        B, N, L, D, H = (8, 128, 512, 128, 16)
        Bq, Nq, Dm = q.shape
        Lk = k.shape[1]
        Hh = H
        Dh = Dm // Hh
        scale = Dm ** (-0.5)
        qh = (q @ Wq.T).reshape(Bq, Nq, Hh, Dh).transpose(0, 2, 1, 3)
        kh = (k @ Wk.T).reshape(Bq, Lk, Hh, Dh).transpose(0, 2, 1, 3)
        vh = (v @ Wv.T).reshape(Bq, Lk, Hh, Dh).transpose(0, 2, 1, 3)
        attn = jnp.einsum('bhnc,bhlc->bhnl', qh * scale, kh)
        attn = jax.nn.softmax(attn, axis=2)
        attn = attn / jnp.sum(attn, axis=-1, keepdims=True)
        out = jnp.einsum('bhnl,bhlc->bhnc', attn, vh)
        out = out.transpose(0, 2, 1, 3).reshape(Bq, Nq, Dm)
        return out @ Wo.T

    def _L0_ffn_ref(x, w_g, c_fc, c_proj):
        import jax, jax.numpy as jnp
        import numpy as np
        import math
        N_EXP = 8
        TOP_K = 2
        CAPACITY_FACTOR = 1.25

        def _capacity(num_tokens):
            cap = math.floor(TOP_K * CAPACITY_FACTOR * num_tokens / N_EXP)
            cap += cap % 2
            return int(cap)
        B, C, d = x.shape
        T = B * C
        cap = _capacity(T)
        xt = x.reshape(T, d)
        logits = xt @ w_g
        top_v, top_i = jax.lax.top_k(logits, TOP_K)
        full = jnp.full_like(logits, -jnp.inf)
        full = full.at[jnp.arange(T)[:, None], top_i].set(top_v)
        probs = jax.nn.softmax(full, axis=-1)
        exp_mask = jax.nn.one_hot(top_i, N_EXP, dtype=jnp.int32)
        exp_mask = jnp.transpose(exp_mask, (1, 0, 2))
        exp_rank = jnp.cumsum(exp_mask.reshape(TOP_K * T, N_EXP), axis=0) - 1
        exp_rank = exp_rank.reshape(TOP_K, T, N_EXP)
        exp_mask = exp_mask * (exp_rank < cap).astype(jnp.int32)
        exp_rank = jnp.sum(exp_mask * exp_rank, axis=-1)
        exp_weights = exp_mask.astype(x.dtype) * probs[None]
        rank_oh = jax.nn.one_hot(exp_rank, cap, dtype=x.dtype)
        cb_weight = jnp.einsum('kte,ktc->tec', exp_weights, rank_oh)
        sec_mask = (cb_weight != 0).astype(x.dtype)
        exp_batches = jnp.einsum('tec,td->ecd', sec_mask, xt)
        h = jax.nn.gelu(jnp.einsum('ecd,edf->ecf', exp_batches, c_fc), approximate=False)
        exp_out = jnp.einsum('ecf,efd->ecd', h, c_proj)
        out = cb_weight.reshape(T, N_EXP * cap) @ exp_out.reshape(N_EXP * cap, d)
        return out.reshape(B, C, d)
    x = _layernorm(x + _L0_attn_ref(x, L0_attn_Wq, L0_attn_Wk, L0_attn_Wv, L0_attn_Wo, L0_attn_bo), axis=-1)
    x = _layernorm(x + _L0_xattn_ref(x, ctx_1024, ctx_1024, L0_xattn_Wq, L0_xattn_Wk, L0_xattn_Wv, L0_xattn_Wo), axis=-1)
    x = _layernorm(x + _L0_ffn_ref(x, L0_ffn_w_g, L0_ffn_c_fc, L0_ffn_c_proj), axis=-1)
    return x

_drawn_inputs = setup_inputs


def setup_inputs(seed=0):
    import zlib

    import numpy as np

    out = dict(_drawn_inputs(seed))
    spreads = {'L0_attn_bo': (0.0, 0.1)}
    factors = {'L0_attn_Wq': 8.0, 'L0_attn_Wk': 8.0, 'L0_attn_Wv': 4.829, 'L0_attn_Wo': 4.712}
    for name, (base, spread) in spreads.items():
        noise = np.random.default_rng([zlib.crc32(name.encode()), seed]).standard_normal(out[name].shape)
        drawn = base * np.exp(spread * noise) if base else spread * noise
        out[name] = jnp.asarray(drawn.astype(out[name].dtype))
    for name, factor in factors.items():
        out[name] = (out[name] * factor).astype(out[name].dtype)
    return out
```

```python
from contextlib import ExitStack

import concourse.bass as bass
from concourse import mybir

F32 = mybir.dt.float32
BF16 = mybir.dt.bfloat16
U32 = mybir.dt.uint32
ALU = mybir.AluOpType
ACT = mybir.ActivationFunctionType
AX = mybir.AxisListType

P = 128
HEADS = 16
PAIRS = HEADS // 2
PART_OF_Q = [0, 0, 0, 1, 1, 1, 2, 2]
PART_OF_K = [0, 1, 2, 0, 1, 2, 0, 1]
TERMS = len(PART_OF_Q)
PARTS = 3
BANK = 512
TILE_COLS = 32
EPS = 1e-5


def decoder_layer(nc, xT, x, ctxT, attn_wqT, attn_wkT, attn_wvT, attn_woT, attn_bo,
                  x_wqT, x_wkT, x_wvT, x_woT, w_g, c_fc, c_proj, out):
    B, S, D = x.shape
    L = ctxT.shape[2]
    E = w_g.shape[1]
    F = c_fc.shape[2]
    HD = D // HEADS
    ROWS = 2 * HD
    QT, LT = S // P, L // P
    T = B * S
    TT = T // P
    TOPK = 2
    CAP = int(TOPK * 1.25 * T / E)
    CAP += CAP % 2
    SLOTS = E * CAP
    ST = SLOTS // P
    FT = F // P
    SELF_SCALE = float(HD) ** -0.5
    CROSS_SCALE = float(D) ** -0.5
    GENERAL = 3
    RING = 4
    PV_AT = [2, 3, 4, 5]
    CROSS_OUT = 7
    UNITS = LT * PAIRS
    assert D == P and ROWS * TERMS == P and S == 256 and SLOTS % P == 0 and FT * P == F
    CV = HD + 1

    PRODUCT_ON_DVE = {("B", 0, 0), ("E", 0, 0)}
    prologue = [
        ("A", 0, 0), ("A", 0, 1), ("B", 0, 0), ("B", 0, 1), ("ck", 0, 0), ("C", 0, 0), ("D", 0, 0),
        ("A", 1, 0), ("E", 0, 0), ("C", 0, 1), ("D", 0, 1), ("E", 0, 1), ("F", 0, 0), ("A", 1, 1), ("cv", 0, 0),
        ("B", 1, 0), ("F", 0, 1), ("B", 1, 1), ("C", 1, 0), ("D", 1, 0),
        ("N4", 0, 0), ("N5", 0, 0), ("E", 1, 0), ("N9", 0, 0), ("N10", 0, 0),
        ("C", 1, 1), ("D", 1, 1), ("E", 1, 1), ("F", 1, 0), ("ck", 1, 0), ("cv", 1, 0), ("F", 1, 1),
    ]

    def beside(i):
        rows = [[] for _ in range(UNITS)]
        if i >= 1:
            for n, k in enumerate(["C2", "C4", "C5", "C9", "C10"]):
                rows[CROSS_OUT + 2 * n].append((k, i - 1, 0))
        if i + 1 < B:
            for n, k in enumerate(["N4", "N5", "N9", "N10"]):
                rows[2 + 3 * n].append((k, i + 1, 0))
        b = i + 2
        if b < B:
            for n, k in enumerate([("A", 0), ("B", 0), ("A", 1), ("B", 1), ("C", 0), ("D", 0), ("E", 0), ("C", 1),
                                   ("D", 1), ("E", 1), ("F", 0), ("F", 1)]):
                rows[4 + 2 * n].append((k[0], b, k[1]))
            rows[29].append(("ck", b, 0))
            rows[30].append(("cv", b, 0))
        return rows

    bodies = [beside(i) for i in range(B)]
    last_norm = [(k, B - 1, 0) for k in ["C2", "C4", "C5", "C9", "C10"]]
    steps = prologue + [x for rows in bodies for row in rows for x in row] + last_norm
    use_list = [x for x in steps if x[0] not in ("B", "C", "D", "E", "F")]
    use_no = {x: n for n, x in enumerate(use_list)}
    split_order = [{"ck": "ck", "N10": "cq"}[k] + str(b) for k, b, _ in steps if k in ("ck", "N10")]

    ctx = ExitStack()
    with ctx:
        def sb(name, shape, dt=F32):
            return ctx.enter_context(nc.sbuf_tensor(name, shape, dt))

        def sem(name):
            return ctx.enter_context(nc.semaphore(name))

        wqkv = sb("wqkv", [P, 3 * D])
        woT = sb("woT", [P, D])
        cwqT = sb("cwqT", [P, D]); cwkT = sb("cwkT", [P, D]); cwvT = sb("cwvT", [P, D]); cwoT = sb("cwoT", [P, D])
        bo = sb("bo", [P, D])
        wg = sb("wg", [P, E])
        xT_sb = sb("xT_sb", [P, B, S])
        cT_sb = sb("cT_sb", [P, B, L])
        x_sb = sb("x_sb", [P, B, QT, D])
        fc = sb("fc", [P, E, F])
        proj = sb("proj", [P, 2, L])
        rest = sb("rest", [P, 2, L])
        parts = sb("parts", [P, 2, PARTS, L], BF16)
        zero = sb("zero", [2 * PARTS, HD * S], BF16)
        zrow = sb("zrow", [P, SLOTS * D // P // 4])
        qkv = sb("qkv", [P, RING, 3 * D])
        prod = sb("prod", [P, 2, HEADS * HEADS * HD])
        sS = sb("sS", [P, 2, HEADS * HEADS])
        sP = sb("sP", [P, 2, HEADS * HEADS])
        smx = sb("smx", [P, 2, HEADS])
        ssum = sb("ssum", [P, 2, HEADS])
        srec = sb("srec", [P, 2, HEADS])
        sOn = sb("sOn", [P, 2, D])
        sO = sb("sO", [P, 2, D])
        cQ = sb("cQ", [P, 2, HEADS, S], BF16)
        cK = sb("cK", [P, 2, PAIRS, L], BF16)
        vOne = sb("vOne", [P, B, LT, HEADS, CV])
        cV = sb("cV", [P, 2, HEADS, TILE_COLS])
        cE = sb("cE", [P, 2, HEADS, S])
        cmx = sb("cmx", [P, 2, 2, PAIRS])
        csum = sb("csum", [P, 2, HEADS])
        crec = sb("crec", [P, 2, HEADS])
        oSb = sb("oSb", [P, BANK])
        oRec = sb("oRec", [P, 2 * HEADS])   
        pj = sb("pj", [P, E, FT, D])
        aN = sb("aN", [P, 2, QT, D])
        aT = sb("aT", [P, 2, S])
        pre = sb("pre", [P, 2, QT, D])
        stats = sb("stats", [P, 2, QT, 6])
        mv = sb("mv", [P, 2, QT, 2])
        rstd = sb("rstd", [P, 2, QT])
        vare = sb("vare", [P, 2, QT])
        half = sb("half", [P, 2 * TT])
        x1 = sb("x1", [P, B, QT, D])
        x1T = sb("x1T", [P, S])
        x2 = sb("x2", [P, TT, D])
        x2T = sb("x2T", [P, S])
        ident = sb("ident", [P, P])
        logits = sb("logits", [P, TT, E])
        top = sb("top", [P, TT, 8])
        topi = sb("topi", [P, TT, 8], U32)
        ef = sb("ef", [P, TOPK, TT])
        iotaE = sb("iotaE", [P, E])
        hot = sb("hot", [P, TOPK, TT, E])
        hotb = sb("hotb", [P, TOPK, TT, E], BF16)
        lower = sb("lower", [P, P], BF16)
        ones = sb("ones", [P, P], BF16)
        total = sb("total", [P, E, TOPK * TT])
        incl = sb("incl", [P, E, TOPK * TT])
        keepgo = sb("keepgo", [P, E, TOPK * TT])
        rank = sb("rank", [P, TOPK * TT, E])
        pos = sb("pos", [P, TOPK * TT])
        keep = sb("keep", [P, TOPK * TT])
        slotf = sb("slotf", [P, TOPK * TT])
        slotg = sb("slotg", [P, TOPK * TT])
        slot = sb("slot", [P, TOPK * TT], U32)
        slotr = sb("slotr", [P, TOPK * TT], U32)
        dz = sb("dz", [P, TT])
        ez = sb("ez", [P, TT])
        ez1 = sb("ez1", [P, TT])
        w = sb("w", [P, TOPK, TT])
        cE_flat = cE[:, :, :, :].rearrange("p a h t -> p (a h t)")
        xs = cE_flat[:, 0:ST * D].rearrange("p (t d) -> p t d", d=D)
        xsT = cE_flat[:, SLOTS:2 * SLOTS]
        hT = cE_flat[:, 2 * SLOTS:2 * SLOTS + 2 * FT * CAP].rearrange("p (a f c) -> p a f c", a=2, f=FT)
        assert 2 * SLOTS + 2 * FT * CAP <= 2 * HEADS * S and TOPK * TT * D <= 2 * HEADS * HEADS * HD
        ys = sb("ys", [P, 2, 3, D])
        yg = prod[:, :, :].rearrange("p a x -> p (a x)")[:, 0:TOPK * TT * D].rearrange("p (c d) -> p c d", d=D)
        res = xT_sb[:, :, :].rearrange("p b t -> p (b t)").rearrange("p (t d) -> p t d", d=D)
        fin = cT_sb[:, :, :].rearrange("p b t -> p (b t)")[:, 0:T].rearrange("p (t d) -> p t d", d=D)
        fstats = sb("fstats", [P, TT, 6])
        fmv = sb("fmv", [P, TT, 2])
        fvar = sb("fvar", [P, TT])
        frstd = sb("frstd", [P, TT])

        cS = [ctx.enter_context(nc.psum_tensor(f"cS{i}", [P, BANK], F32)) for i in range(4)]
        gB = [ctx.enter_context(nc.psum_tensor(f"gB{i}", [P, BANK], F32)) for i in range(GENERAL)]
        oC = ctx.enter_context(nc.psum_tensor("oC", [P, BANK], F32))

        q_scr = nc.dram_tensor("q_scr", (2, PARTS, HEADS, ROWS, S), BF16, kind="Internal").ap()
        ck_scr = nc.dram_tensor("ck_scr", (B, PARTS, P, L), BF16, kind="Internal").ap()
        a_scr = nc.dram_tensor("a_scr", (B, HEADS, S, HD), F32, kind="Internal").ap()
        xs_d = nc.dram_tensor("xs_d", (SLOTS, D), F32, kind="Internal").ap()
        ys_d = nc.dram_tensor("ys_d", (SLOTS, D), F32, kind="Internal").ap()

        wqkv_in = sem("wqkv_in"); w_in = sem("w_in"); x_in = [sem("x_in0"), sem("x_in1")]; c_in = [sem("c_in0"), sem("c_in1")]; res_in = sem("res_in"); moe_in = sem("moe_in")
        zeroed = sem("zeroed")
        consts = sem("consts")
        cchain = sem("cchain")
        bias_added = sem("bias_added")
        pads = sem("pads")
        pad_dma = sem("pad_dma")
        xs_zero = sem("xs_zero")
        g_ready = sem("g_ready")
        proj_out = sem("proj_out")
        split = sem("split")
        parts_out = [sem("parts_out0"), sem("parts_out1")]
        ck_in = [sem("ck_in0"), sem("ck_in1")]
        cq_in = [sem("cq_in0"), sem("cq_in1")]
        cv_out = sem("cv_out")
        qkv_out = sem("qkv_out")
        qk_done = [sem("qk_done0"), sem("qk_done1")]
        s_step = sem("s_step")
        s_ready = sem("s_ready")
        p_done = sem("p_done")
        pv_done = [sem("pv_done0"), sem("pv_done1")]
        srec_done = sem("srec_done")
        f_done = sem("f_done")
        a_st = [sem("a_st0"), sem("a_st1")]
        a_in = sem("a_in")
        c_pv = sem("c_pv")
        cs_ready = sem("cs_ready")
        cm_done = sem("cm_done")
        cE_done = sem("cE_done")
        crec_done = sem("crec_done")
        cV_done = sem("cV_done")
        o_out = sem("o_out")
        rec_done = sem("rec_done")
        a_done = sem("a_done")
        at_done = [sem("at_doneS"), sem("at_doneC")]
        pre_done = [sem("pre_doneS"), sem("pre_doneC")]
        st_done = [sem("st_doneS"), sem("st_doneC")]
        mv_done = [sem("mv_doneS"), sem("mv_doneC")]
        pow_step = [sem("pow_stepS"), sem("pow_stepC")]
        ln_done = [sem("ln_doneS"), sem("ln_doneC")]
        xt_done = [sem("xt_doneS"), sem("xt_doneC")]
        log_done = sem("log_done")
        chain = sem("chain")
        route = sem("route")
        ex_done = sem("ex_done")
        rank_mm = sem("rank_mm")
        slot_done = sem("slot_done")
        scat = sem("scat"); xs_in = sem("xs_in")
        xt_mm = sem("xt_mm"); xt_cp = sem("xt_cp")
        h_mm = sem("h_mm"); gelu = sem("gelu"); y_mm = sem("y_mm"); y_cp = sem("y_cp")
        ys_out = [sem("ys_out0"), sem("ys_out1")]
        gath = sem("gath")
        f_chain = sem("f_chain"); f_var = sem("f_var"); f_pow = sem("f_pow"); f_ln = sem("f_ln")
        stored = sem("stored")
        block = ctx.enter_context(nc.Block())

        def uno(kind, b=0, n=0):
            return use_no[(kind, b, n)]

        def bank(kind, b=0, n=0):
            return gB[uno(kind, b, n) % GENERAL]

        def await_use(eng, kind, b=0, n=0):
            eng.wait_ge(g_ready, uno(kind, b, n) + 1)

        def read(kind, b, n):
            if kind == "A":
                return qkv_out, b * QT + n + 1
            if kind == "cv":
                return cv_out, b + 1
            if kind == "ck":
                return proj_out, split_no("ck", b) + 1
            if kind == "N10":
                return proj_out, split_no("cq", b) + 1
            return {"C2": a_done, "N4": at_done[0], "C4": at_done[1], "N5": pre_done[0], "C5": pre_done[1],
                    "N9": xt_done[0], "C9": xt_done[1], "C10": log_done}[kind], b + 1

        def split_no(kind, b):
            return split_order.index(kind + str(b))

        def split_len(kind):
            return L if kind == "ck" else S

        parts_count = {}
        cnt = [0, 0]
        for n, name in enumerate(split_order):
            cnt[n % 2] += 16 * (2 * PARTS if name[:2] == "cq" else PARTS)
            parts_count[name] = cnt[n % 2]

        def product(eng, api, k, b, q):
            if (eng is nc.vector) != ((k, b, q) in PRODUCT_ON_DVE):
                return
            n = b * QT + q
            if k == "B":
                eng.wait_ge(qkv_out, n + 1)
                if n >= 2:
                    eng.wait_ge(f_done, n - 1)
                api.tensor_tensor(
                    out=prod[:, n % 2, :].rearrange("p (a k d) -> p a k d", a=HEADS, d=HD),
                    in0=qkv[:, n % RING, 0:D].rearrange("p (a d) -> p a d", d=HD).unsqueeze(2)
                    .to_broadcast([P, HEADS, HEADS, HD]),
                    in1=qkv[:, n % RING, D:2 * D].rearrange("p (k d) -> p k d", d=HD).unsqueeze(1)
                    .to_broadcast([P, HEADS, HEADS, HD]), op=ALU.mult).then_inc(qk_done[n % 2], 1)
            else:
                eng.wait_ge(p_done, n + 1)
                api.tensor_tensor(
                    out=prod[:, n % 2, :].rearrange("p (a d k) -> p a d k", a=HEADS, d=HD),
                    in0=sP[:, n % 2, :].rearrange("p (a k) -> p a k", a=HEADS).unsqueeze(2)
                    .to_broadcast([P, HEADS, HD, HEADS]),
                    in1=qkv[:, n % RING, 2 * D:3 * D].rearrange("p (k d) -> p d k", d=HD).unsqueeze(1)
                    .to_broadcast([P, HEADS, HD, HEADS]), op=ALU.mult).then_inc(pv_done[n % 2], 1)

        @block.sync
        def _(sp):
            sp.dma_start(xT_sb[:, 0, :], xT[:, 0, :]).then_inc(x_in[0], 16)
            for n, src in enumerate((attn_wqT, attn_wkT, attn_wvT)):
                sp.dma_start(wqkv[:, n * D:(n + 1) * D], src).then_inc(wqkv_in, 16)
            sp.dma_start(cwkT[:, :], x_wkT).then_inc(c_in[0], 16)
            sp.dma_start(cwvT[:, :], x_wvT).then_inc(c_in[0], 16)
            sp.dma_start(cT_sb[:, 0, :], ctxT[:, 0, :]).then_inc(c_in[0], 16)
            sp.dma_start(xT_sb[:, 1:B, :], xT[:, 1:B, :]).then_inc(x_in[1], 16)
            for dst, src in ((woT, attn_woT), (cwqT, x_wqT), (cwoT, x_woT), (wg, w_g)):
                sp.dma_start(dst[:, :], src).then_inc(w_in, 16)
            sp.dma_start(bo[:, :], attn_bo.partition_broadcast(P)).then_inc(res_in, 16)
            sp.dma_start(x_sb[:, :, :, :], x.rearrange("b (q p) d -> p b q d", p=P)).then_inc(res_in, 16)
            sp.wait_ge(zeroed, 1)
            for hf in range(2):
                sp.dma_start(
                    q_scr[:, :, hf * PAIRS:(hf + 1) * PAIRS, (1 - hf) * HD:(2 - hf) * HD, :]
                    .rearrange("b p j d t -> (b p) j (d t)"),
                    zero[:, :].unsqueeze(1).to_broadcast([2 * PARTS, PAIRS, HD * S])).then_inc(pad_dma, 16)
            sp.dma_start(cT_sb[:, 1:B, :], ctxT[:, 1:B, :]).then_inc(c_in[1], 16)

            def write_parts(kind, b):
                n = split_no(kind, b)
                for p in range(PARTS):
                    sp.wait_ge(split, 4 * n + (1, 3, 4)[p])
                    if kind == "cq":
                        if p == 0 and b >= 2:
                            sp.wait_ge(cq_in[b % 2], 16 * TERMS * (b // 2))
                        for hf in range(2):
                            sp.dma_start(
                                q_scr[b % 2, p, hf * PAIRS:(hf + 1) * PAIRS, hf * HD:(hf + 1) * HD, :]
                                .rearrange("j d t -> j (d t)"),
                                parts[hf * 64:(hf + 1) * 64, n % 2, p, 0:S]).then_inc(parts_out[n % 2], 16)
                    else:
                        sp.dma_start(ck_scr[b, p], parts[:, n % 2, p, 0:L]).then_inc(parts_out[n % 2], 16)

            def read_stack(kind, b):
                n = split_no(kind, b)
                sp.wait_ge(parts_out[n % 2], parts_count[kind + str(b)])
                if b == 0 and kind == "cq":
                    sp.wait_ge(pad_dma, 32)
                if b >= 2:
                    sp.wait_ge(cs_ready, UNITS * (b - 1))
                for t in range(TERMS):
                    rows = slice(ROWS * t, ROWS * (t + 1))
                    if kind == "cq":
                        sp.dma_start(cQ[rows, b % 2, :, :], q_scr[b % 2, PART_OF_Q[t]].rearrange("h r t -> r h t")
                                     ).then_inc(cq_in[b % 2], 16)
                    else:
                        sp.dma_start(cK[rows, b % 2, :, :],
                                     ck_scr[b, PART_OF_K[t]].rearrange("(j r) t -> r j t", r=ROWS)
                                     ).then_inc(ck_in[b % 2], 16)

            def work(row):
                for k, b, q in row:
                    if k == "ck":
                        write_parts("ck", b)
                        read_stack("ck", b)
                    elif k == "N10":
                        write_parts("cq", b)
                        read_stack("cq", b)
                    elif k == "F":
                        n = b * QT + q
                        sp.wait_ge(f_done, n + 1)
                        sp.dma_start(a_scr[b, :, q * P:(q + 1) * P, :].rearrange("h s d -> s h d"),
                                     sO[:, n % 2, :].rearrange("p (h d) -> p h d", d=HD)).then_inc(a_st[q], 16)
                    elif k == "N4":
                        for q in range(QT):
                            sp.wait_ge(a_st[q], 16 * (b + 1))
                        if b >= 1:
                            await_use(sp, "N4", b - 1)
                        sp.dma_start(aN[:, 0, :, :], a_scr[b].rearrange("h (r x) d -> (h r) (x d)", x=HEADS)
                                     .rearrange("(q p) c -> p q c", p=P)).then_inc(a_in, 16)

            work(prologue)
            sp.dma_start(fc[:, :, :], c_fc.rearrange("e d f -> d e f")).then_inc(moe_in, 16)
            sp.dma_start(pj.rearrange("p e a d -> p (e a) d"), c_proj.rearrange("e (a f) d -> f (e a) d", f=P)
                         ).then_inc(moe_in, 16)
            sp.wait_ge(zeroed, 2)
            for q in range(4):
                sp.dma_start(xs_d[q * SLOTS // 4:(q + 1) * SLOTS // 4, :].rearrange("(p r) d -> p (r d)", p=P),
                             zrow[:, :]).then_inc(xs_zero, 16)
            for rows in bodies:
                for row in rows:
                    work(row)
            sp.wait_ge(scat, 16 * TOPK * TT)
            sp.dma_start(xs[:, :, :], xs_d.rearrange("(t p) d -> p t d", p=P)).then_inc(xs_in, 16)
            for e in range(E):
                sp.wait_ge(y_cp, e + 1)
                for c in range(3):
                    n = min(P, CAP - c * P)
                    sp.dma_start(ys_d[e * CAP + c * P:e * CAP + c * P + n, :], ys[0:n, e % 2, c, :]
                                 ).then_inc(ys_out[e % 2], 16)
            for t in range(TT):
                sp.wait_ge(f_ln, t + 1)
                sp.dma_start(out.rearrange("b (q p) d -> (b q) p d", p=P)[t], fin[:, t, :]).then_inc(stored, 16)
            sp.wait_ge(stored, 16 * TT)

        @block.gpsimd
        def _(pool):
            pool.memset(half[:, :], -0.5).then_inc(consts, 1)
            made = [0]

            def step(ins):
                made[0] += 1
                ins.then_inc(cchain, 1)
                pool.wait_ge(cchain, made[0])

            step(pool.memset(ident[:, :], 0.0))
            step(pool.affine_select(out=ident[:, :], in_=ident[:, :], compare_op=ALU.not_equal, fill=1.0,
                                    base=0, pattern=[[-1, P]], channel_multiplier=1))
            def split_parts(kind, b):
                n = split_no(kind, b)
                m = split_len(kind)
                src, r, pt = proj[:, n % 2, 0:m], rest[:, n % 2, 0:m], parts[:, n % 2]
                pool.wait_ge(proj_out, n + 1)
                if n >= 2:
                    pool.wait_ge(parts_out[n % 2], parts_count[split_order[n - 2]])
                pool.tensor_scalar(pt[:, 0, 0:m], src, 1.0, 1.0, ALU.mult, ALU.mult).then_inc(split, 1)
                pool.wait_ge(split, 4 * n + 1)
                pool.tensor_tensor(out=r, in0=src, in1=pt[:, 0, 0:m], op=ALU.subtract).then_inc(split, 1)
                pool.wait_ge(split, 4 * n + 2)
                pool.tensor_scalar(pt[:, 1, 0:m], r, 1.0, 1.0, ALU.mult, ALU.mult).then_inc(split, 1)
                pool.wait_ge(split, 4 * n + 3)
                pool.tensor_tensor(out=pt[:, 2, 0:m], in0=r, in1=pt[:, 1, 0:m], op=ALU.subtract).then_inc(split, 1)

            def power(a, b):
                pool.wait_ge(mv_done[a], QT * (b + 1))
                if b >= 1:
                    pool.wait_ge(ln_done[a], QT * b)
                pool.tensor_scalar(vare[:, a, :], mv[:, a, :, 1], EPS, 1.0, ALU.add, ALU.mult).then_inc(pow_step[a], 1)
                pool.wait_ge(pow_step[a], 2 * b + 1)
                pool.tensor_tensor(out=rstd[:, a, :], in0=vare[:, a, :], in1=half[:, 0:QT], op=ALU.pow
                                   ).then_inc(pow_step[a], 1)

            def scale_v(b, lt):
                n = b * LT + lt
                pool.wait_ge(crec_done, n + 1)
                pool.wait_ge(cv_out, b + 1)
                if n >= 2:
                    pool.wait_ge(c_pv, n - 1)
                for s in range(2):
                    v = vOne[:, b, lt].rearrange("p (c s) d -> p c s d", s=2)[:, :, s, :]
                    o = cV[:, n % 2].rearrange("p (c s) d -> p c s d", s=2)[:, :, s, s * CV:(s + 1) * CV]
                    r = crec[:, n % 2].rearrange("p (c s) -> p c s", s=2)[:, :, s:s + 1]
                    pool.tensor_tensor(out=o, in0=v, in1=r.to_broadcast([P, HEADS // 2, CV]), op=ALU.mult
                                       ).then_inc(cV_done, 1)

            def work(row):
                for k, b, n in row:
                    if k == "ck":
                        split_parts("ck", b)
                    elif k == "N4" and b == 0:
                        pool.wait_ge(res_in, 32)
                        pool.tensor_tensor(out=x_sb[:, :, :, :].rearrange("p b q d -> p (b q) d"),
                                           in0=x_sb[:, :, :, :].rearrange("p b q d -> p (b q) d"),
                                           in1=bo[:, :].unsqueeze(1).to_broadcast([P, B * QT, D]), op=ALU.add
                                           ).then_inc(bias_added, 1)
                    elif k in "BE":
                        product(pool, nc.gpsimd, k, b, n)
                    elif k == "N9":
                        power(0, b)
                    elif k == "C9":
                        power(1, b)
                    elif k == "N10":
                        split_parts("cq", b)

            pool.wait_ge(pads, 2)
            work(prologue)
            step(pool.memset(ones[:, :], 1.0))
            step(pool.affine_select(out=lower[:, :], in_=ones[:, :], compare_op=ALU.is_gt, fill=0.0,
                                    base=0, pattern=[[1, P]], channel_multiplier=-1))
            step(pool.iota(iotaE[:, :], pattern=[[1, E]], base=0, channel_multiplier=0,
                           allow_small_or_imprecise_dtypes=True))
            step(pool.memset(keepgo[:, :, 1:TOPK * TT], 1.0))
            pool.memset(keepgo[:, :, 0:1], 0.0).then_inc(consts, 1)
            for i in range(B):
                for s in range(UNITS):
                    if s % PAIRS == 1 and (i or s >= PAIRS):
                        n = i * LT + s // PAIRS - 1
                        scale_v(n // LT, n % LT)
                    work(bodies[i][s])
            scale_v(B - 1, LT - 1)
            work(last_norm)
            pool.wait_ge(slot_done, 1)
            pool.wait_ge(xs_zero, 16 * 4)
            for k in range(TOPK):
                for t in range(TT):
                    c = k * TT + t
                    pool.indirect_dma_start(
                        out=xs_d, out_offset=bass.IndirectOffsetOnAxis(ap=slot[:, c:c + 1], axis=0),
                        in_=x2[:, t, :], in_offset=None, bounds_check=SLOTS - 1, oob_is_err=False).then_inc(scat, 16)
            pool.wait_ge(ys_out[0], 16 * 3 * (E // 2))
            pool.wait_ge(ys_out[1], 16 * 3 * (E // 2))
            for t in range(TT):
                for k in range(TOPK):
                    c = k * TT + t
                    pool.indirect_dma_start(
                        out=yg[:, c, :], out_offset=None, in_=ys_d,
                        in_offset=bass.IndirectOffsetOnAxis(ap=slotr[:, c:c + 1], axis=0),
                        bounds_check=SLOTS - 1, oob_is_err=False).then_inc(gath, 16)
            for t in range(TT):
                pool.wait_ge(f_var, t + 1)
                pool.tensor_tensor(out=frstd[:, t:t + 1], in0=fvar[:, t:t + 1], in1=half[:, 0:1], op=ALU.pow
                                   ).then_inc(f_pow, 1)

        @block.tensor
        def _(pe):
            mm = nc.tensor.matmul

            def begin(kind, b=0, n=0):
                u = uno(kind, b, n)
                if u >= GENERAL:
                    pe.wait_ge(*read(*use_list[u - GENERAL]))
                return gB[u % GENERAL]

            def project(kind, b, q):
                g = begin(kind, b, q)
                if kind == "A":
                    pe.wait_ge(x_in[min(b, 1)], 16)
                    pe.wait_ge(wqkv_in, 48)
                    last = mm(g[:, 0:3 * D], xT_sb[:, b, q * P:(q + 1) * P], wqkv[:, :], start=True, stop=True)
                elif kind == "ck":
                    pe.wait_ge(c_in[0], 48)
                    if b >= 1:
                        pe.wait_ge(c_in[1], 16)
                    last = mm(g[:, 0:L], cwkT[:, :], cT_sb[:, b, :], start=True, stop=True)
                else:
                    for q in range(LT):
                        last = mm(g[:, q * D:(q + 1) * D], cT_sb[:, b, q * P:(q + 1) * P], cwvT[:, :],
                                  start=True, stop=True)
                last.then_inc(g_ready, 1)

            def place(h):
                return h // PAIRS, (h % PAIRS) // 2

            def cross_scores(b, u):
                lt, j = u // PAIRS, u % PAIRS
                n = b * UNITS + u
                if u == 0:
                    pe.wait_ge(ck_in[b % 2], 16 * TERMS * (b // 2 + 1))
                    pe.wait_ge(cq_in[b % 2], 16 * TERMS * (b // 2 + 1))
                if n >= 4:
                    pe.wait_ge(cE_done, n - 3)
                mm(cS[n % 4][:, :], cK[:, b % 2, j, lt * P:(lt + 1) * P],
                   cQ[:, b % 2, j:j + PAIRS + 1:PAIRS, :], start=True, stop=True).then_inc(cs_ready, 1)

            def cross_pv(b, lt, i):
                n = b * LT + lt
                if i == 0:
                    pe.wait_ge(cV_done, 2 * (n + 1))
                    if lt == 0 and b >= 1:
                        pe.wait_ge(o_out, b)
                first = PAIRS * (i // 4) + 4 * (i % 2) + i % 4 // 2
                for h in (first, first + 2):
                    r, c = place(h)
                    last = mm(oC[TILE_COLS * c:TILE_COLS * (c + 1), r * S:(r + 1) * S],
                              cV[:, n % 2, h, :], cE[:, n % 2, h, :],
                              start=(lt == 0 and r == 0 and h % 2 == 0),
                              stop=(lt == LT - 1 and r == 1 and h % 2 == 1), skip_group_check=True)
                if i == PAIRS - 1:
                    last.then_inc(c_pv, 1)

            def norm_step(a, k, b):
                kind = "NC"[a] + k
                if k == "2":
                    g = begin(kind, b)
                    pe.wait_ge(o_out, b + 1)
                    for q in range(QT):
                        for r in range(2):
                            last = nc.tensor.transpose(g[:, (q * 2 + r) * P:(q * 2 + r + 1) * P],
                                                       oSb[:, r * S + q * P:r * S + (q + 1) * P], ident[:, :])
                elif k == "4":
                    g = begin(kind, b)
                    if a == 0:
                        pe.wait_ge(a_in, 16 * (b + 1))
                    else:
                        pe.wait_ge(a_done, b + 1)
                    for q in range(QT):
                        last = nc.tensor.transpose(g[:, q * P:(q + 1) * P], aN[:, a, q, :], ident[:, :])
                elif k == "5":
                    g = begin(kind, b)
                    pe.wait_ge(w_in, 16 * 4)
                    pe.wait_ge(at_done[a], b + 1)
                    for q in range(QT):
                        last = mm(g[:, q * D:(q + 1) * D], aT[:, a, q * P:(q + 1) * P],
                                  (woT, cwoT)[a][:, :], start=True, stop=True)
                elif k == "9":
                    g = begin(kind, b)
                    pe.wait_ge(ln_done[a], QT * (b + 1))
                    for q in range(QT):
                        src = x1[:, b, q, :] if a == 0 else x2[:, b * QT + q, :]
                        last = nc.tensor.transpose(g[:, q * P:(q + 1) * P], src, ident[:, :])
                elif a == 0:
                    g = begin(kind, b)
                    pe.wait_ge(xt_done[0], b + 1)
                    last = mm(g[:, 0:S], cwqT[:, :], x1T[:, :], start=True, stop=True)
                else:
                    g = begin(kind, b)
                    pe.wait_ge(xt_done[1], b + 1)
                    for q in range(QT):
                        last = mm(g[:, q * E:(q + 1) * E], x2T[:, q * P:(q + 1) * P], wg[:, :],
                                  start=True, stop=True)
                last.then_inc(g_ready, 1)

            def work(row):
                for k, b, n in row:
                    if k in ("A", "ck", "cv"):
                        project(k, b, n)
                    elif k[0] in "NC" and len(k) > 1:
                        norm_step("NC".index(k[0]), k[1:], b)

            pe.wait_ge(cchain, 2)
            work(prologue)
            AHEAD = 2
            for i in range(B):
                for s in range(UNITS):
                    if i == 0 and s == 0:
                        for a in range(AHEAD):
                            cross_scores(0, a)
                    n = i * UNITS + s + AHEAD
                    if n < B * UNITS:
                        cross_scores(n // UNITS, n % UNITS)
                    work(bodies[i][s])
                    n = i * LT + s // PAIRS - 1
                    if n >= 0 and s % PAIRS in PV_AT:
                        for k in range(2):
                            cross_pv(n // LT, n % LT, 2 * PV_AT.index(s % PAIRS) + k)
            for k in range(PAIRS):
                cross_pv(B - 1, LT - 1, k)
            work(last_norm)

            pe.wait_ge(route, 1)
            pe.wait_ge(cE_done, B * UNITS)
            m_ = hotb[:, :, :, :].rearrange("p k t e -> p (k t e)")
            mm(cS[0][:, 0:TOPK * TT * E], lower[:, :], m_, start=True, stop=True)
            mm(cS[1][:, 0:TOPK * TT * E], ones[:, :], m_, start=True, stop=True).then_inc(rank_mm, 1)
            pe.wait_ge(xs_in, 16)
            pe.wait_ge(slot_done, 1)
            for n in range(ST // 4):
                if n >= 2:
                    pe.wait_ge(xt_cp, n - 1)
                for c in range(4):
                    last = nc.tensor.transpose(cS[n % 2][:, c * P:(c + 1) * P], xs[:, 4 * n + c, :], ident[:, :])
                last.then_inc(xt_mm, 1)
            pe.wait_ge(moe_in, 32)

            def up(e):
                pe.wait_ge(xt_cp, (min((e + 1) * CAP, SLOTS) + 4 * P - 1) // (4 * P))
                for f in range(FT):
                    n = e * FT + f
                    if n >= 4:
                        pe.wait_ge(gelu, n - 3)
                    mm([cS[2], cS[3], gB[0], gB[1]][n % 4][:, 0:CAP], fc[:, e, f * P:(f + 1) * P],
                       xsT[:, e * CAP:(e + 1) * CAP], start=True, stop=True).then_inc(h_mm, 1)

            def down(e):
                pe.wait_ge(gelu, FT * (e + 1))
                if e >= 2:
                    pe.wait_ge(y_cp, e - 1)
                for c in range(3):
                    n = min(P, CAP - c * P)
                    for f in range(FT):
                        last = mm([gB[2], oC][e % 2][0:n, c * D:(c + 1) * D], hT[:, e % 2, f, c * P:c * P + n],
                                  pj[:, e, f, :], start=(f == 0), stop=(f == FT - 1))
                last.then_inc(y_mm, 1)

            pe.wait_ge(log_done, B)
            up(0)
            for e in range(E):
                if e + 1 < E:
                    up(e + 1)
                down(e)

        @block.scalar
        def _(act):
            A = nc.scalar.activation

            def copy_proj(kind, b, use):
                n = split_no(kind, b)
                if n >= 2:
                    act.wait_ge(split, 4 * (n - 1))
                await_use(act, *use)
                scale = CROSS_SCALE if kind == "cq" else 1.0
                m = split_len(kind)
                ins = A(proj[:, n % 2, 0:m], bank(*use)[:, 0:m], ACT.Copy, scale=scale)
                ins.then_inc(proj_out, 1)

            def work(row):
                for k, b, n in row:
                    if k == "ck":
                        copy_proj("ck", b, (k, b, 0))
                    elif k == "N10":
                        copy_proj("cq", b, (k, b, 0))
                    elif k == "A":
                        await_use(act, k, b, n)
                        m = b * QT + n
                        if m >= RING:
                            act.wait_ge(pv_done[m % 2], (m - RING) // 2 + 1)
                        A(qkv[:, m % RING, :], bank(k, b, n)[:, 0:3 * D], ACT.Copy).then_inc(qkv_out, 1)
                    elif k == "D":
                        m = b * QT + n
                        act.wait_ge(s_ready, m + 1)
                        if m >= 2:
                            act.wait_ge(f_done, m - 1)
                        A(sP[:, m % 2, :], sS[:, m % 2, :], ACT.Exp, scale=SELF_SCALE).then_inc(p_done, 1)

            work(prologue)
            for i in range(B):
                for s in range(UNITS):
                    n = i * UNITS + s
                    lt, j = s // PAIRS, s % PAIRS
                    g = i * LT + lt
                    act.wait_ge(cm_done, n + 1)
                    if j == 0 and g >= 2:
                        act.wait_ge(c_pv, g - 1)
                        act.wait_ge(crec_done, g - 1)
                    for hf in range(2):
                        ins = A(cE[:, g % 2, hf * PAIRS + j, :], cS[n % 4][:, hf * S:(hf + 1) * S], ACT.Exp,
                                bias=cmx[:, g % 2, hf, j:j + 1],
                                accum_out=csum[:, g % 2, hf * PAIRS + j:hf * PAIRS + j + 1])
                    ins.then_inc(cE_done, 1)
                    work(bodies[i][s])
            act.wait_ge(chain, 3)
            A(ez[:, :], dz[:, :], ACT.Exp).then_inc(ex_done, 1)
            for n in range(E * FT):
                e, f = n // FT, n % FT
                act.wait_ge(h_mm, n + 1)
                if e >= 2:
                    act.wait_ge(y_mm, e - 1)
                A(hT[:, e % 2, f, :], [cS[2], cS[3], gB[0], gB[1]][n % 4][:, 0:CAP], ACT.Gelu).then_inc(gelu, 1)

        @block.vector
        def _(dve):
            V = nc.vector
            V.memset(zero[:, :], 0.0).then_inc(zeroed, 1)
            V.memset(cV[:, :, :, :], 0.0).then_inc(pads, 1)
            V.memset(zrow[:, :], 0.0).then_inc(zeroed, 1)
            V.memset(vOne[:, :, :, :, :], 1.0).then_inc(pads, 1)

            steps_done = [0]

            def after(ins):
                steps_done[0] += 1
                ins.then_inc(s_step, 1)
                dve.wait_ge(s_step, steps_done[0])

            def self_step(k, b, q):
                n = b * QT + q
                m = n % 2
                S_ = sS[:, m, :].rearrange("p (a k) -> p a k", a=HEADS)
                if k == "C":
                    dve.wait_ge(qk_done[m], n // 2 + 1)
                    after(V.tensor_reduce(out=sS[:, m, :], in_=prod[:, m, :].rearrange("p (s d) -> p s d", d=HD),
                                          axis=AX.X, op=ALU.add))
                    after(V.tensor_reduce(out=smx[:, m, :], in_=S_, axis=AX.X, op=ALU.max))
                    V.tensor_tensor(out=S_, in0=S_, in1=smx[:, m, :].unsqueeze(2).to_broadcast([P, HEADS, HEADS]),
                                    op=ALU.subtract).then_inc(s_ready, 1)
                elif k == "E":
                    dve.wait_ge(p_done, n + 1)
                    after(V.tensor_reduce(out=ssum[:, m, :], in_=sP[:, m, :].rearrange("p (a k) -> p a k", a=HEADS),
                                          axis=AX.X, op=ALU.add))
                    V.reciprocal(srec[:, m, :], ssum[:, m, :]).then_inc(srec_done, 1)
                elif k == "F":
                    dve.wait_ge(pv_done[m], n // 2 + 1)
                    dve.wait_ge(srec_done, n + 1)
                    if n >= 2:
                        dve.wait_ge(a_st[q], 16 * b)
                    after(V.tensor_reduce(out=sOn[:, m, :], in_=prod[:, m, :].rearrange("p (s k) -> p s k", k=HEADS),
                                          axis=AX.X, op=ALU.add))
                    V.tensor_tensor(out=sO[:, m, :].rearrange("p (a d) -> p a d", d=HD),
                                    in0=sOn[:, m, :].rearrange("p (a d) -> p a d", d=HD),
                                    in1=srec[:, m, :].unsqueeze(2).to_broadcast([P, HEADS, HD]), op=ALU.mult
                                    ).then_inc(f_done, 1)

            def copy_v(b):
                await_use(dve, "cv", b)
                dve.wait_ge(pads, 2)
                V.tensor_copy(vOne[:, b].rearrange("p l h d -> p (l h) d")[:, :, 0:HD],
                              bank("cv", b)[:, 0:LT * D].rearrange("p (lh d) -> p lh d", d=HD)).then_inc(cv_out, 1)

            def sums(g):
                dve.wait_ge(cE_done, PAIRS * (g + 1))
                if g >= 2:
                    dve.wait_ge(cV_done, 2 * (g - 1))
                V.reciprocal(crec[:, g % 2, :], csum[:, g % 2, :]).then_inc(crec_done, 1)

            def evacuate_sums(b):
                dve.wait_ge(c_pv, LT * (b + 1))
                if b >= 1:
                    await_use(dve, "C2", b - 1)
                V.tensor_copy(oSb[:, :], oC[:, :]).then_inc(o_out, 1)

            def norm_step(a, k, b):
                kind = "NC"[a] + k
                await_use(dve, kind, b)
                g = bank(kind, b)
                if k == "2":
                    t = g[:, :].rearrange("p (c x) -> p c x", x=TILE_COLS)[:, :, 0:2 * CV] \
                        .rearrange("p c (s d) -> p c s d", s=2)
                    r = oRec[:, :].rearrange("p (c s) -> p c s", s=2)
                    V.reciprocal(r, t[:, :, :, HD]).then_inc(rec_done, 1)
                    dve.wait_ge(rec_done, b + 1)
                    ins = V.tensor_tensor(
                        out=aN[:, a].rearrange("p q (c s d) -> p (q c) s d", s=2, d=HD), in0=t[:, :, :, 0:HD],
                        in1=r.unsqueeze(3).to_broadcast([P, HEADS, 2, HD]), op=ALU.mult)
                    ins.then_inc(a_done, 1)
                elif k == "4":
                    ins = V.tensor_copy(aT[:, a, :], g[:, 0:S])
                    ins.then_inc(at_done[a], 1)
                elif k == "5":
                    if a == 0 and b == 0:
                        dve.wait_ge(bias_added, 1)
                    src = x_sb[:, b] if a == 0 else x1[:, b]
                    ins = V.tensor_tensor(out=pre[:, a].rearrange("p q d -> p (q d)"), in0=g[:, 0:QT * D],
                                          in1=src.rearrange("p q d -> p (q d)"), op=ALU.add)
                    ins.then_inc(pre_done[a], 1)
                elif k == "9":
                    ins = V.tensor_copy((x1T, x2T)[a][:, :], g[:, 0:S])
                    ins.then_inc(xt_done[a], 1)
                else:
                    ins = V.tensor_copy(logits[:, b * QT:(b + 1) * QT, :].rearrange("p q e -> p (q e)"),
                                        g[:, 0:QT * E])
                    ins.then_inc(log_done, 1)

            def layer_norm(a, b):
                dve.wait_ge(pre_done[a], b + 1)
                for q in range(QT):
                    V.bn_stats(stats[:, a, q, :], pre[:, a, q, :]).then_inc(st_done[a], 1)
                for q in range(QT):
                    dve.wait_ge(st_done[a], QT * b + q + 1)
                    V.bn_aggr(mv[:, a, q, :], stats[:, a, q, :]).then_inc(mv_done[a], 1)

            def normalise(a, b):
                dve.wait_ge(pow_step[a], 2 * (b + 1))
                for q in range(QT):
                    dst = x1[:, b, q, :] if a == 0 else x2[:, b * QT + q, :]
                    V.tensor_scalar(dst, pre[:, a, q, :], mv[:, a, q, 0:1], rstd[:, a, q:q + 1],
                                    ALU.subtract, ALU.mult).then_inc(ln_done[a], 1)

            def work(row):
                for k, b, n in row:
                    if k == "cv":
                        copy_v(b)
                    elif k in "BCEF":
                        if k in "BE":
                            product(dve, V, k, b, n)
                        self_step(k, b, n)
                    elif k[0] in "NC":
                        a = "NC".index(k[0])
                        if k == "N10":
                            continue
                        if k == "N9" and b >= 1:
                            await_use(dve, "N10", b - 1)
                        if k[1:] == "9":
                            normalise(a, b)
                        norm_step(a, k[1:], b)
                        if k[1:] == "5":
                            layer_norm(a, b)

            work(prologue)
            for i in range(B):
                for s in range(UNITS):
                    n = i * UNITS + s
                    lt, j = s // PAIRS, s % PAIRS
                    g = i * LT + lt
                    dve.wait_ge(cs_ready, n + 1)
                    if g >= 2 and j == 0:
                        dve.wait_ge(cE_done, PAIRS * (g - 1))
                    V.tensor_reduce(out=cmx[:, g % 2, :, j], in_=cS[n % 4][:, :].rearrange("p (a t) -> p a t", a=2),
                                    axis=AX.X, op=ALU.max, negate=True).then_inc(cm_done, 1)
                    if s % PAIRS == 1 and g >= 1:
                        sums(g - 1)
                    if s == CROSS_OUT - 1 and i >= 1:
                        evacuate_sums(i - 1)
                    work(bodies[i][s])
            sums(B * LT - 1)
            evacuate_sums(B - 1)
            work(last_norm)

            count = [0]

            def link(ins):
                count[0] += 1
                ins.then_inc(chain, 1)
                dve.wait_ge(chain, count[0])

            dve.wait_ge(log_done, B)
            for t in range(TT):
                ins = V.max(top[:, t, :], logits[:, t, :])
            link(ins)
            for t in range(TT):
                ins = V.max_index(topi[:, t, :], top[:, t, :], logits[:, t, :])
            link(ins)
            link(V.tensor_tensor(out=dz[:, :], in0=top[:, :, 1], in1=top[:, :, 0], op=ALU.subtract))
            link(V.tensor_copy(ef[:, :, :], topi[:, :, 0:TOPK].rearrange("p t k -> p k t")))
            dve.wait_ge(consts, 2)
            link(V.tensor_tensor(out=hot[:, :, :, :].rearrange("p k t e -> p (k t) e"),
                                 in0=ef[:, :, :].rearrange("p k t -> p (k t)").unsqueeze(2)
                                 .to_broadcast([P, TOPK * TT, E]),
                                 in1=iotaE[:, :].unsqueeze(1).to_broadcast([P, TOPK * TT, E]), op=ALU.is_equal))
            V.tensor_copy(hotb[:, :, :, :], hot[:, :, :, :]).then_inc(route, 1)
            dve.wait_ge(ex_done, 1)
            link(V.tensor_scalar(ez1[:, :], ez[:, :], 1.0, None, ALU.add))
            link(V.reciprocal(w[:, 0, :], ez1[:, :]))
            link(V.tensor_tensor(out=w[:, 1, :], in0=w[:, 0, :], in1=ez[:, :], op=ALU.mult))
            dve.wait_ge(rank_mm, 1)
            KT = TOPK * TT
            link(V.tensor_copy(total[:, :, :], cS[1][:, 0:KT * E].rearrange("p (kt e) -> p e kt", e=E)))
            link(V.tensor_tensor_scan(out=incl[:, :, :].rearrange("p e k -> p (e k)"),
                                      data0=keepgo[:, :, :].rearrange("p e k -> p (e k)"),
                                      data1=total[:, :, :].rearrange("p e k -> p (e k)"),
                                      initial=0.0, op0=ALU.mult, op1=ALU.add))
            link(V.tensor_tensor(out=total[:, :, :], in0=incl[:, :, :], in1=total[:, :, :], op=ALU.subtract))
            link(V.tensor_tensor(out=rank[:, :, :], in0=cS[0][:, 0:KT * E].rearrange("p (kt e) -> p kt e", e=E),
                                 in1=total[:, :, :].rearrange("p e k -> p k e"), op=ALU.add))
            link(V.tensor_tensor(out=rank[:, :, :], in0=rank[:, :, :],
                                 in1=hot[:, :, :, :].rearrange("p k t e -> p (k t) e"), op=ALU.mult))
            link(V.tensor_reduce(out=pos[:, :], in_=rank[:, :, :], axis=AX.X, op=ALU.add))
            link(V.tensor_scalar(keep[:, :], pos[:, :], float(CAP), None, ALU.is_lt))
            link(V.scalar_tensor_tensor(out=slotf[:, :], in0=ef[:, :, :].rearrange("p k t -> p (k t)"),
                                        scalar=float(CAP), in1=pos[:, :], op0=ALU.mult, op1=ALU.add))
            link(V.tensor_tensor(out=slotg[:, :], in0=slotf[:, :], in1=keep[:, :], op=ALU.mult))
            link(V.tensor_copy(slotr[:, :], slotg[:, :]))
            link(V.tensor_scalar(slotf[:, :], keep[:, :], -float(SLOTS), float(SLOTS), ALU.mult, ALU.add))
            link(V.tensor_tensor(out=slotf[:, :], in0=slotf[:, :], in1=slotg[:, :], op=ALU.add))
            V.tensor_copy(slot[:, :], slotf[:, :]).then_inc(slot_done, 1)
            link(V.tensor_tensor(out=w[:, :, :].rearrange("p k t -> p (k t)"),
                                 in0=w[:, :, :].rearrange("p k t -> p (k t)"), in1=keep[:, :], op=ALU.mult))
            for n in range(ST // 4):
                dve.wait_ge(xt_mm, n + 1)
                V.tensor_copy(xsT[:, n * 4 * P:(n + 1) * 4 * P], cS[n % 2][:, :]).then_inc(xt_cp, 1)
            for e in range(E):
                dve.wait_ge(y_mm, e + 1)
                if e >= 2:
                    dve.wait_ge(ys_out[e % 2], 16 * 3 * (e // 2))
                V.tensor_copy(ys[:, e % 2, 0:2, :].rearrange("p c d -> p (c d)"), [gB[2], oC][e % 2][:, 0:2 * D])
                V.tensor_copy(ys[0:CAP - 2 * P, e % 2, 2, :], [gB[2], oC][e % 2][0:CAP - 2 * P, 2 * D:3 * D]
                              ).then_inc(y_cp, 1)
            fc_n = [0]

            def flink(ins):
                fc_n[0] += 1
                ins.then_inc(f_chain, 1)
                dve.wait_ge(f_chain, fc_n[0])

            def finish(t):
                dve.wait_ge(f_pow, t + 1)
                V.tensor_scalar(fin[:, t, :], res[:, t, :], fmv[:, t, 0:1], frstd[:, t:t + 1],
                                ALU.subtract, ALU.mult).then_inc(f_ln, 1)

            for t in range(TT):
                dve.wait_ge(gath, 16 * TOPK * TT)
                flink(V.scalar_tensor_tensor(out=res[:, t, :], in0=yg[:, t, :], scalar=w[:, 0, t:t + 1],
                                             in1=x2[:, t, :], op0=ALU.mult, op1=ALU.add))
                flink(V.scalar_tensor_tensor(out=res[:, t, :], in0=yg[:, TT + t, :], scalar=w[:, 1, t:t + 1],
                                             in1=res[:, t, :], op0=ALU.mult, op1=ALU.add))
                flink(V.bn_stats(fstats[:, t, :], res[:, t, :]))
                flink(V.bn_aggr(fmv[:, t, :], fstats[:, t, :]))
                V.tensor_scalar(fvar[:, t:t + 1], fmv[:, t, 1:2], EPS, None, ALU.add).then_inc(f_var, 1)
                if t >= 1:
                    finish(t - 1)
            finish(TT - 1)


def kernel(x, ctx_1024, L0_attn_Wq, L0_attn_Wk, L0_attn_Wv, L0_attn_Wo, L0_attn_bo,
           L0_xattn_Wq, L0_xattn_Wk, L0_xattn_Wv, L0_xattn_Wo, L0_ffn_w_g, L0_ffn_c_fc, L0_ffn_c_proj):
    import numpy as np
    import concourse.bacc as bacc
    from concourse.bass_utils import run_bass_kernel_spmd

    def columns_by_pair(w):
        d = w.shape[1]
        return w.T.reshape(d, 2, PAIRS, d // HEADS).transpose(0, 2, 1, 3).reshape(d, d)

    a = np.asarray
    arrays = {
        "xT": a(x).transpose(2, 0, 1), "x": a(x), "ctxT": a(ctx_1024).transpose(2, 0, 1),
        "attn_wqT": a(L0_attn_Wq).T, "attn_wkT": a(L0_attn_Wk).T,
        "attn_wvT": a(L0_attn_Wv).T, "attn_woT": a(L0_attn_Wo).T, "attn_bo": a(L0_attn_bo),
        "x_wqT": a(L0_xattn_Wq).T, "x_wkT": columns_by_pair(a(L0_xattn_Wk)),
        "x_wvT": a(L0_xattn_Wv).T, "x_woT": a(L0_xattn_Wo).T,
        "w_g": a(L0_ffn_w_g), "c_fc": a(L0_ffn_c_fc), "c_proj": a(L0_ffn_c_proj),
    }
    arrays = {k: np.ascontiguousarray(v) for k, v in arrays.items()}
    nc = bacc.Bacc("TRN2", target_bir_lowering=False, num_devices=1)
    args = [nc.dram_tensor(k, v.shape, mybir.dt.from_np(v.dtype), kind="ExternalInput").ap()
            for k, v in arrays.items()]
    out = nc.dram_tensor("out", a(x).shape, F32, kind="ExternalOutput").ap()
    decoder_layer(nc, *args, out)
    r = run_bass_kernel_spmd(nc, [arrays], core_ids=[0])
    return r.results[0]["out"]
```

```python
from contextlib import ExitStack

import concourse.bass as bass
from concourse import mybir

F32 = mybir.dt.float32
BF16 = mybir.dt.bfloat16
U32 = mybir.dt.uint32
ALU = mybir.AluOpType
ACT = mybir.ActivationFunctionType
AX = mybir.AxisListType

P = 128
HEADS = 16
PAIRS = HEADS // 2
PART_OF_Q = [0, 0, 0, 1, 1, 1, 2, 2]
PART_OF_K = [0, 1, 2, 0, 1, 2, 0, 1]
TERMS = len(PART_OF_Q)
PARTS = 3
BANK = 512
TILE_COLS = 32
EPS = 1e-5


def decoder_layer(nc, xT, x, ctxT, attn_wqT, attn_wkT, attn_wvT, attn_woT, attn_bo,
                  x_wqT, x_wkT, x_wvT, x_woT, w_g, c_fc, c_proj, out):
    B, S, D = x.shape
    L = ctxT.shape[2]
    E = w_g.shape[1]
    F = c_fc.shape[2]
    HD = D // HEADS
    ROWS = 2 * HD
    QT, LT = S // P, L // P
    T = B * S
    TT = T // P
    TOPK = 2
    CAP = int(TOPK * 1.25 * T / E)
    CAP += CAP % 2
    SLOTS = E * CAP
    ST = SLOTS // P
    FT = F // P
    SELF_SCALE = float(HD) ** -0.5
    CROSS_SCALE = float(D) ** -0.5
    GENERAL = 3
    RING = 4
    PV_AT = [2, 3, 4, 5]
    CROSS_OUT = 7
    ZEROS = 4
    NONE = 4 * T
    RW = D + 1
    UNITS = LT * PAIRS
    assert D == P and ROWS * TERMS == P and S == 256 and SLOTS % P == 0 and FT * P == F
    CV = HD + 1

    PRODUCT_ON_DVE = {("B", 0, 0), ("E", 0, 0)}
    prologue = [
        ("A", 0, 0), ("A", 0, 1), ("B", 0, 0), ("B", 0, 1), ("C", 0, 0), ("D", 0, 0), ("ck", 0, 0), ("cv", 0, 0),
        ("in", 1, 0), ("C", 0, 1), ("D", 0, 1), ("E", 0, 0), ("E", 0, 1), ("A", 1, 0), ("A", 1, 1), ("F", 0, 0),
        ("F", 0, 1), ("B", 1, 0), ("N4", 0, 0), ("C", 1, 0), ("D", 1, 0), ("N5", 0, 0), ("N9", 0, 0), ("N10", 0, 0),
        ("B", 1, 1), ("C", 1, 1), ("D", 1, 1), ("in", 2, 0), ("ck", 1, 0), ("cv", 1, 0),
    ]

    def beside(i):
        rows = [[] for _ in range(UNITS)]
        if i >= 1:
            for n, k in enumerate(["C2", "C4", "C5", "C9", "C10"]):
                rows[CROSS_OUT + 2 * n].append((k, i - 1, 0))
            rows[CROSS_OUT + 11].append(("R", i - 1, 0))
        if i + 1 < B:
            for s, k, q in ((0, "E", 0), (1, "E", 1), (5, "F", 0), (10, "F", 1), (14, "N4", 0), (16, "N5", 0),
                            (19, "N9", 0), (20, "N10", 0)):
                rows[s].append((k, i + 1, q))
        if i + 2 < B:
            for s, k, q in ((9, "A", 0), (10, "A", 1), (10, "B", 0), (15, "B", 1), (17, "C", 0), (18, "D", 0),
                            (23, "C", 1), (24, "D", 1), (27, "ck", 0), (28, "cv", 0)):
                rows[s].append((k, i + 2, q))
        if i + 3 < B:
            rows[21].append(("in", i + 3, 0))
        if i == 0:
            for n in range(2 * ZEROS):
                rows[4 * n + 3].append(("z", n, 0))
        if i in (1, 2):
            for n in range(E):
                rows[4 * n + 3].append(("w", E * (i - 1) + n, 0))
        return rows

    bodies = [beside(i) for i in range(B)]
    last_norm = [(k, B - 1, 0) for k in ["C2", "C4", "C5", "C9", "C10", "R"]]
    steps = prologue + [x for rows in bodies for row in rows for x in row] + last_norm
    use_list = [x for x in steps if x[0] not in ("B", "C", "D", "E", "F", "in", "w", "z")]
    use_no = {x: n for n, x in enumerate(use_list)}
    split_order = [{"ck": "ck", "N10": "cq"}[k] + str(b) for k, b, _ in steps if k in ("ck", "N10")]

    ctx = ExitStack()
    with ctx:
        def sb(name, shape, dt=F32):
            return ctx.enter_context(nc.sbuf_tensor(name, shape, dt))

        def sem(name):
            return ctx.enter_context(nc.semaphore(name))

        wqkv = sb("wqkv", [P, 3 * D])
        woT = sb("woT", [P, D])
        cwqT = sb("cwqT", [P, D]); cwkT = sb("cwkT", [P, D]); cwvT = sb("cwvT", [P, D]); cwoT = sb("cwoT", [P, D])
        bo = sb("bo", [P, D])
        wg = sb("wg", [P, E])
        xT_sb = sb("xT_sb", [P, B, S])
        cT_sb = sb("cT_sb", [P, B, L])
        x_sb = sb("x_sb", [P, B, QT, D])
        fc = sb("fc", [P, E, F])
        proj = sb("proj", [P, 2, L])
        rest = sb("rest", [P, 2, L])
        parts = sb("parts", [P, 2, PARTS, L], BF16)
        zero = sb("zero", [2 * PARTS, HD * S], BF16)
        zrow = sb("zrow", [P, SLOTS * RW // P // ZEROS])
        qkv = sb("qkv", [P, RING, 3 * D])
        prod = sb("prod", [P, 2, HEADS * HEADS * HD])
        sS = sb("sS", [P, 2, HEADS * HEADS])
        sP = sb("sP", [P, 2, HEADS * HEADS])
        smx = sb("smx", [P, 2, HEADS])
        ssum = sb("ssum", [P, 2, HEADS])
        srec = sb("srec", [P, 2, HEADS])
        sOn = sb("sOn", [P, 2, D])
        sO = sb("sO", [P, 2, D])
        cQ = sb("cQ", [P, 2, HEADS, S], BF16)
        cK = sb("cK", [P, 2, PAIRS, L], BF16)
        vOne = sb("vOne", [P, B, LT, HEADS, CV])
        cV = sb("cV", [P, 2, HEADS, TILE_COLS])
        cE = sb("cE", [P, 2, HEADS, S])
        cmx = sb("cmx", [P, 2, 2, PAIRS])
        csum = sb("csum", [P, 2, HEADS])
        crec = sb("crec", [P, 2, HEADS])
        oSb = sb("oSb", [P, BANK])
        oRec = sb("oRec", [P, 2 * HEADS])   
        pj = sb("pj", [P, E, FT, D])
        aN = sb("aN", [P, 2, QT, D])
        aT = sb("aT", [P, 2, S])
        pre = sb("pre", [P, 2, QT, D])
        stats = sb("stats", [P, 2, QT, 6])
        mv = sb("mv", [P, 2, QT, 2])
        vare = sb("vare", [P, 2, QT])
        half = sb("half", [P, 2])
        rstd = sb("rstd", [P, 2, QT])
        x1 = sb("x1", [P, B, QT, D])
        x1T = sb("x1T", [P, S])
        x2 = sb("x2", [P, TT, RW])
        x2T = sb("x2T", [P, S])
        ident = sb("ident", [P, P])
        logits = sb("logits", [P, TT, E])
        top = sb("top", [P, TT, 8])
        topi = sb("topi", [P, TT, 8], U32)
        ef = sb("ef", [P, TOPK, TT])
        iotaE = sb("iotaE", [P, E])
        hotb = sb("hotb", [P, TOPK, TT, E], BF16)
        before = sb("before", [P, TOPK, TT + 1, E], BF16)
        lower = sb("lower", [P, P], BF16)
        ones = sb("ones", [P, P], BF16)
        rank = sb("rank", [P, TOPK * TT, E])
        pos = sb("pos", [P, TOPK * TT])
        keep = sb("keep", [P, TOPK * TT])
        over = sb("over", [P, TOPK * TT])
        slotf = sb("slotf", [P, TOPK * TT])
        slot = sb("slot", [P, TOPK * TT], U32)
        row_of = sb("row_of", [P, E, 3], U32)
        dz = sb("dz", [P, TT])
        ez = sb("ez", [P, TT])
        ez1 = sb("ez1", [P, TT])
        w = sb("w", [P, TOPK, TT])
        cE_flat = cE[:, :, :, :].rearrange("p a h t -> p (a h t)")
        XS = 3 * E * RW
        xs = cE_flat[:, 0:XS].rearrange("p (e c d) -> p e c d", e=E, d=RW)
        xsT = cE_flat[:, XS:XS + SLOTS]
        yg = cE_flat[:, XS + SLOTS:XS + SLOTS + TOPK * TT * D].rearrange("p (c d) -> p c d", d=D)
        hT = prod[:, :, :].rearrange("p a x -> p (a x)")[:, 0:3 * FT * CAP].rearrange(
            "p (a f c) -> p a f c", a=3, f=FT)
        assert XS + SLOTS + TOPK * TT * D <= 2 * HEADS * S and 3 * FT * CAP <= 2 * HEADS * HEADS * HD
        ys = sb("ys", [P, 2, 3, D])
        res = xT_sb[:, :, :].rearrange("p b t -> p (b t)").rearrange("p (t d) -> p t d", d=D)
        fin = cT_sb[:, :, :].rearrange("p b t -> p (b t)")[:, 0:T].rearrange("p (t d) -> p t d", d=D)
        fstats = sb("fstats", [P, TT, 6])
        fmv = sb("fmv", [P, TT, 2])
        fvare = sb("fvare", [P, TT])
        frstd = sb("frstd", [P, TT])

        cS = [ctx.enter_context(nc.psum_tensor(f"cS{i}", [P, BANK], F32)) for i in range(4)]
        gB = [ctx.enter_context(nc.psum_tensor(f"gB{i}", [P, BANK], F32)) for i in range(GENERAL)]
        oC = ctx.enter_context(nc.psum_tensor("oC", [P, BANK], F32))

        q_scr = nc.dram_tensor("q_scr", (2, PARTS, HEADS, ROWS, S), BF16, kind="Internal").ap()
        ck_scr = nc.dram_tensor("ck_scr", (B, PARTS, P, L), BF16, kind="Internal").ap()
        a_scr = nc.dram_tensor("a_scr", (B, HEADS, S, HD), F32, kind="Internal").ap()
        xs_d = nc.dram_tensor("xs_d", (SLOTS, RW), F32, kind="Internal").ap()
        yg_d = nc.dram_tensor("yg_d", (TOPK * T, D), F32, kind="Internal").ap()

        wqkv_in = sem("wqkv_in"); w_in = sem("w_in"); 
        x_in = [sem(f"x_in{b}") for b in range(B)]
        c_in = [sem(f"c_in{b}") for b in range(B)]
        res_in = [sem(f"res_in{b}") for b in range(B)]
        cw_in = sem("cw_in")
        moe_in = sem("moe_in")
        zeroed = sem("zeroed")
        consts = sem("consts")
        cchain = sem("cchain")
        bias_added = sem("bias_added")
        pads = sem("pads")
        pad_dma = sem("pad_dma")
        xs_zero = sem("xs_zero")
        g_ready = sem("g_ready")
        proj_out = sem("proj_out")
        split = sem("split")
        parts_out = [sem("parts_out0"), sem("parts_out1")]
        ck_in = [sem("ck_in0"), sem("ck_in1")]
        cq_in = [sem("cq_in0"), sem("cq_in1")]
        cv_out = sem("cv_out")
        qkv_out = sem("qkv_out")
        qk_done = [sem("qk_done0"), sem("qk_done1")]
        s_step = sem("s_step")
        s_ready = sem("s_ready")
        p_done = sem("p_done")
        pv_done = [sem("pv_done0"), sem("pv_done1")]
        srec_done = sem("srec_done")
        f_done = sem("f_done")
        a_st = [sem("a_st0"), sem("a_st1")]
        a_in = sem("a_in")
        c_pv = sem("c_pv")
        cs_ready = sem("cs_ready")
        cm_done = sem("cm_done")
        cE_done = sem("cE_done")
        crec_done = sem("crec_done")
        cV_done = sem("cV_done")
        o_out = sem("o_out")
        rec_done = sem("rec_done")
        a_done = sem("a_done")
        at_done = [sem("at_doneS"), sem("at_doneC")]
        pre_done = [sem("pre_doneS"), sem("pre_doneC")]
        st_done = [sem("st_doneS"), sem("st_doneC")]
        mv_done = [sem("mv_doneS"), sem("mv_doneC")]
        vare_done = [sem("vare_doneS"), sem("vare_doneC")]
        rstd_done = [sem("rstd_doneS"), sem("rstd_doneC")]
        ln_done = [sem("ln_doneS"), sem("ln_doneC")]
        xt_done = [sem("xt_doneS"), sem("xt_doneC")]
        log_done = sem("log_done")
        chain = sem("chain")
        route = sem("route")
        dz_done = sem("dz_done")
        ex_done = sem("ex_done")
        rank_read = sem("rank_read")
        slot_done = sem("slot_done")
        scat = [sem("scat0"), sem("scat1"), sem("scat2")]
        xs_in = [sem(f"xs_in{e}") for e in range(E)]
        xt_mm = sem("xt_mm"); xt_cp = sem("xt_cp")
        rows_done = sem("rows_done")
        h_mm = sem("h_mm"); gelu = sem("gelu"); y_mm = sem("y_mm"); y_cp = sem("y_cp")
        ys_out = [sem("ys_out0"), sem("ys_out1")]
        gath = [sem("gath0"), sem("gath1")]
        f_chain = sem("f_chain"); f_vare = sem("f_vare"); f_rstd = sem("f_rstd"); f_ln = sem("f_ln")
        stored = sem("stored")
        block = ctx.enter_context(nc.Block())

        def uno(kind, b=0, n=0):
            return use_no[(kind, b, n)]

        def bank(kind, b=0, n=0):
            return gB[uno(kind, b, n) % GENERAL]

        def await_use(eng, kind, b=0, n=0):
            eng.wait_ge(g_ready, uno(kind, b, n) + 1)

        def read(kind, b, n):
            if kind == "A":
                return qkv_out, b * QT + n + 1
            if kind == "cv":
                return cv_out, b + 1
            if kind == "ck":
                return proj_out, split_no("ck", b) + 1
            if kind == "N10":
                return proj_out, split_no("cq", b) + 1
            return {"C2": a_done, "N4": at_done[0], "C4": at_done[1], "N5": pre_done[0], "C5": pre_done[1],
                    "N9": xt_done[0], "C9": xt_done[1], "C10": log_done, "R": rank_read}[kind], b + 1

        def split_no(kind, b):
            return split_order.index(kind + str(b))

        def split_len(kind):
            return L if kind == "ck" else S

        parts_count = {}
        cnt = [0, 0]
        for n, name in enumerate(split_order):
            cnt[n % 2] += 16 * (2 * PARTS if name[:2] == "cq" else PARTS)
            parts_count[name] = cnt[n % 2]

        def product(eng, api, k, b, q):
            if (eng is nc.vector) != ((k, b, q) in PRODUCT_ON_DVE):
                return
            n = b * QT + q
            if k == "B":
                eng.wait_ge(qkv_out, n + 1)
                if n >= 2:
                    eng.wait_ge(f_done, n - 1)
                api.tensor_tensor(
                    out=prod[:, n % 2, :].rearrange("p (a k d) -> p a k d", a=HEADS, d=HD),
                    in0=qkv[:, n % RING, 0:D].rearrange("p (a d) -> p a d", d=HD).unsqueeze(2)
                    .to_broadcast([P, HEADS, HEADS, HD]),
                    in1=qkv[:, n % RING, D:2 * D].rearrange("p (k d) -> p k d", d=HD).unsqueeze(1)
                    .to_broadcast([P, HEADS, HEADS, HD]), op=ALU.mult).then_inc(qk_done[n % 2], 1)
            else:
                eng.wait_ge(p_done, n + 1)
                api.tensor_tensor(
                    out=prod[:, n % 2, :].rearrange("p (a d k) -> p a d k", a=HEADS, d=HD),
                    in0=sP[:, n % 2, :].rearrange("p (a k) -> p a k", a=HEADS).unsqueeze(2)
                    .to_broadcast([P, HEADS, HD, HEADS]),
                    in1=qkv[:, n % RING, 2 * D:3 * D].rearrange("p (k d) -> p d k", d=HD).unsqueeze(1)
                    .to_broadcast([P, HEADS, HD, HEADS]), op=ALU.mult).then_inc(pv_done[n % 2], 1)

        @block.sync
        def _(sp):
            sp.dma_start(xT_sb[:, 0, :], xT[:, 0, :]).then_inc(x_in[0], 16)
            for n, src in enumerate((attn_wqT, attn_wkT, attn_wvT)):
                sp.dma_start(wqkv[:, n * D:(n + 1) * D], src).then_inc(wqkv_in, 16)
            sp.dma_start(cwkT[:, :], x_wkT).then_inc(cw_in, 16)
            sp.dma_start(cwvT[:, :], x_wvT).then_inc(cw_in, 16)
            sp.dma_start(cT_sb[:, 0, :], ctxT[:, 0, :]).then_inc(c_in[0], 16)
            sp.dma_start(bo[:, :], attn_bo.partition_broadcast(P)).then_inc(res_in[0], 16)
            sp.dma_start(x_sb[:, 0, :, :], x[0].rearrange("(q p) d -> p q d", p=P)).then_inc(res_in[0], 16)
            for dst, src in ((woT, attn_woT), (cwqT, x_wqT), (cwoT, x_woT), (wg, w_g)):
                sp.dma_start(dst[:, :], src).then_inc(w_in, 16)
            sp.wait_ge(zeroed, 1)
            for hf in range(2):
                sp.dma_start(
                    q_scr[:, :, hf * PAIRS:(hf + 1) * PAIRS, (1 - hf) * HD:(2 - hf) * HD, :]
                    .rearrange("b p j d t -> (b p) j (d t)"),
                    zero[:, :].unsqueeze(1).to_broadcast([2 * PARTS, PAIRS, HD * S])).then_inc(pad_dma, 16)

            def write_parts(kind, b):
                n = split_no(kind, b)
                for p in range(PARTS):
                    sp.wait_ge(split, 4 * n + (1, 3, 4)[p])
                    if kind == "cq":
                        if p == 0 and b >= 2:
                            sp.wait_ge(cq_in[b % 2], 16 * TERMS * (b // 2))
                        for hf in range(2):
                            sp.dma_start(
                                q_scr[b % 2, p, hf * PAIRS:(hf + 1) * PAIRS, hf * HD:(hf + 1) * HD, :]
                                .rearrange("j d t -> j (d t)"),
                                parts[hf * 64:(hf + 1) * 64, n % 2, p, 0:S]).then_inc(parts_out[n % 2], 16)
                    else:
                        sp.dma_start(ck_scr[b, p], parts[:, n % 2, p, 0:L]).then_inc(parts_out[n % 2], 16)

            def read_stack(kind, b):
                n = split_no(kind, b)
                sp.wait_ge(parts_out[n % 2], parts_count[kind + str(b)])
                if b == 0 and kind == "cq":
                    sp.wait_ge(pad_dma, 32)
                if b >= 2:
                    sp.wait_ge(cs_ready, UNITS * (b - 1))
                for t in range(TERMS):
                    rows = slice(ROWS * t, ROWS * (t + 1))
                    if kind == "cq":
                        sp.dma_start(cQ[rows, b % 2, :, :], q_scr[b % 2, PART_OF_Q[t]].rearrange("h r t -> r h t")
                                     ).then_inc(cq_in[b % 2], 16)
                    else:
                        sp.dma_start(cK[rows, b % 2, :, :],
                                     ck_scr[b, PART_OF_K[t]].rearrange("(j r) t -> r j t", r=ROWS)
                                     ).then_inc(ck_in[b % 2], 16)

            def work(row):
                for k, b, q in row:
                    if k == "in":
                        sp.dma_start(xT_sb[:, b, :], xT[:, b, :]).then_inc(x_in[b], 16)
                        sp.dma_start(cT_sb[:, b, :], ctxT[:, b, :]).then_inc(c_in[b], 16)
                        sp.dma_start(x_sb[:, b, :, :], x[b].rearrange("(q p) d -> p q d", p=P)).then_inc(res_in[b], 16)
                    elif k == "z":
                        if b == 0:
                            sp.wait_ge(zeroed, 2)
                        n = b % ZEROS
                        dst = (xs_d if b < ZEROS else yg_d).rearrange("(z p r) d -> z p (r d)", z=ZEROS, p=P)[n]
                        sp.dma_start(dst, zrow[:, 0:dst.shape[1]]).then_inc(xs_zero, 16)
                    elif k == "w":
                        e = b // 2
                        if b % 2 == 0:
                            sp.dma_start(fc[:, e, :], c_fc[e]).then_inc(moe_in, 16)
                        else:
                            sp.dma_start(pj[:, e, :, :], c_proj[e].rearrange("(a f) d -> f a d", f=P)
                                         ).then_inc(moe_in, 16)
                    elif k == "ck":
                        write_parts("ck", b)
                        read_stack("ck", b)
                    elif k == "N10":
                        write_parts("cq", b)
                        read_stack("cq", b)
                    elif k == "F":
                        n = b * QT + q
                        sp.wait_ge(f_done, n + 1)
                        sp.dma_start(a_scr[b, :, q * P:(q + 1) * P, :].rearrange("h s d -> s h d"),
                                     sO[:, n % 2, :].rearrange("p (h d) -> p h d", d=HD)).then_inc(a_st[q], 16)
                    elif k == "N4":
                        for q in range(QT):
                            sp.wait_ge(a_st[q], 16 * (b + 1))
                        if b >= 1:
                            await_use(sp, "N4", b - 1)
                        sp.dma_start(aN[:, 0, :, :], a_scr[b].rearrange("h (r x) d -> (h r) (x d)", x=HEADS)
                                     .rearrange("(q p) c -> p q c", p=P)).then_inc(a_in, 16)

            work(prologue)
            for rows in bodies:
                for row in rows:
                    work(row)
            sp.wait_ge(scat[0], 16 * (TT - QT))
            sp.wait_ge(scat[1], 16 * QT)
            sp.wait_ge(scat[2], 16 * TT)
            for e in range(E):
                sp.dma_start(xs[:, e, 0:2, :], xs_d[e * CAP:e * CAP + 2 * P, :].rearrange("(c p) d -> p c d", p=P)
                             ).then_inc(xs_in[e], 16)
                sp.dma_start(xs[0:CAP - 2 * P, e, 2, :], xs_d[e * CAP + 2 * P:(e + 1) * CAP, :]
                             ).then_inc(xs_in[e], 16)
            sp.wait_ge(ys_out[0], 16 * 3 * (E // 2))
            sp.wait_ge(ys_out[1], 16 * 3 * (E // 2))
            for half_ in range(2):
                for k in range(TOPK):
                    c = k * TT + half_ * TT // 2
                    sp.dma_start(yg[:, c:c + TT // 2, :], yg_d[c * P:(c + TT // 2) * P, :]
                                 .rearrange("(t p) d -> p t d", p=P)).then_inc(gath[half_], 16)
            for g in range(TT // 2):
                sp.wait_ge(f_ln, 2 * (g + 1))
                sp.dma_start(out.rearrange("b (q p) d -> p (b q) d", p=P)[:, 2 * g:2 * g + 2, :],
                             fin[:, 2 * g:2 * g + 2, :]).then_inc(stored, 16)
            sp.wait_ge(stored, 16 * (TT // 2))

        @block.gpsimd
        def _(pool):
            pool.memset(half[:, :], -0.5).then_inc(consts, 1)
            made = [0]

            def step(ins):
                made[0] += 1
                ins.then_inc(cchain, 1)
                pool.wait_ge(cchain, made[0])

            step(pool.memset(ident[:, :], 0.0))
            step(pool.affine_select(out=ident[:, :], in_=ident[:, :], compare_op=ALU.not_equal, fill=1.0,
                                    base=0, pattern=[[-1, P]], channel_multiplier=1))
            def split_parts(kind, b):
                n = split_no(kind, b)
                m = split_len(kind)
                src, r, pt = proj[:, n % 2, 0:m], rest[:, n % 2, 0:m], parts[:, n % 2]
                pool.wait_ge(proj_out, n + 1)
                if n >= 2:
                    pool.wait_ge(parts_out[n % 2], parts_count[split_order[n - 2]])
                pool.tensor_scalar(pt[:, 0, 0:m], src, 1.0, 1.0, ALU.mult, ALU.mult).then_inc(split, 1)
                pool.wait_ge(split, 4 * n + 1)
                pool.tensor_tensor(out=r, in0=src, in1=pt[:, 0, 0:m], op=ALU.subtract).then_inc(split, 1)
                pool.wait_ge(split, 4 * n + 2)
                pool.tensor_scalar(pt[:, 1, 0:m], r, 1.0, 1.0, ALU.mult, ALU.mult).then_inc(split, 1)
                pool.wait_ge(split, 4 * n + 3)
                pool.tensor_tensor(out=pt[:, 2, 0:m], in0=r, in1=pt[:, 1, 0:m], op=ALU.subtract).then_inc(split, 1)

            def power(a, b):
                pool.wait_ge(vare_done[a], b + 1)
                if b >= 1:
                    pool.wait_ge(ln_done[a], QT * b)
                pool.tensor_tensor(out=rstd[:, a, :], in0=vare[:, a, :], in1=half[:, 0:QT], op=ALU.pow
                                   ).then_inc(rstd_done[a], 1)

            def scale_v(b, lt):
                n = b * LT + lt
                pool.wait_ge(crec_done, n + 1)
                pool.wait_ge(cv_out, b + 1)
                if n >= 2:
                    pool.wait_ge(c_pv, n - 1)
                for s in range(2):
                    v = vOne[:, b, lt].rearrange("p (c s) d -> p c s d", s=2)[:, :, s, :]
                    o = cV[:, n % 2].rearrange("p (c s) d -> p c s d", s=2)[:, :, s, s * CV:(s + 1) * CV]
                    r = crec[:, n % 2].rearrange("p (c s) -> p c s", s=2)[:, :, s:s + 1]
                    pool.tensor_tensor(out=o, in0=v, in1=r.to_broadcast([P, HEADS // 2, CV]), op=ALU.mult
                                       ).then_inc(cV_done, 1)

            def scatter(k, tiles, done):
                for t in tiles:
                    pool.indirect_dma_start(
                        out=xs_d, out_offset=bass.IndirectOffsetOnAxis(ap=slot[:, k * TT + t:k * TT + t + 1], axis=0),
                        in_=x2[:, t, :], in_offset=None, bounds_check=SLOTS - 1, oob_is_err=False
                    ).then_inc(done, 16)

            def second_rows(tiles, done):
                pool.wait_ge(done, 16 * len(tiles))
                rows = x2[:, tiles[0]:tiles[-1] + 1, D]
                step(pool.tensor_scalar(rows, rows, float(T), 1.0, ALU.add, ALU.mult))

            def work(row):
                for k, b, n in row:
                    if k == "ck":
                        split_parts("ck", b)
                    elif k == "R":
                        early, late = range(QT * (B - 1)), range(QT * (B - 1), TT)
                        if b == B - 1:
                            second_rows(early, scat[0])
                        pool.wait_ge(slot_done, b + 1)
                        if b == 0:
                            pool.wait_ge(xs_zero, 16 * 2 * ZEROS)
                            pool.wait_ge(consts, 2)
                        if b < B - 1:
                            scatter(0, range(QT * b, QT * (b + 1)), scat[0])
                        else:
                            scatter(0, late, scat[1])
                            scatter(1, early, scat[2])
                            second_rows(late, scat[1])
                            scatter(1, late, scat[2])
                    elif k in "BE":
                        product(pool, nc.gpsimd, k, b, n)
                    elif k == "F" and n == 0:
                        pool.wait_ge(res_in[0], 32)
                        if b >= 1:
                            pool.wait_ge(res_in[b], 16)
                        pool.tensor_tensor(out=x_sb[:, b, :, :], in0=x_sb[:, b, :, :],
                                           in1=bo[:, :].unsqueeze(1).to_broadcast([P, QT, D]), op=ALU.add
                                           ).then_inc(bias_added, 1)
                    elif k == "N9":
                        power(0, b)
                    elif k == "C9":
                        power(1, b)
                    elif k == "N10":
                        split_parts("cq", b)

            pool.wait_ge(pads, 2)
            work(prologue)
            step(pool.memset(ones[:, :], 1.0))
            step(pool.affine_select(out=lower[:, :], in_=ones[:, :], compare_op=ALU.is_gt, fill=0.0,
                                    base=0, pattern=[[1, P]], channel_multiplier=-1))
            step(pool.iota(iotaE[:, :], pattern=[[1, E]], base=0, channel_multiplier=0,
                           allow_small_or_imprecise_dtypes=True))
            pool.iota(x2[:, :, D:D + 1], pattern=[[P, TT], [0, 1]], base=-NONE, channel_multiplier=1,
                      allow_small_or_imprecise_dtypes=True).then_inc(consts, 1)
            for i in range(B):
                for s in range(UNITS):
                    if s % PAIRS == 1 and (i or s >= PAIRS):
                        n = i * LT + s // PAIRS - 1
                        scale_v(n // LT, n % LT)
                    work(bodies[i][s])
            scale_v(B - 1, LT - 1)
            work(last_norm)
            for e in range(E):
                pool.wait_ge(y_cp, e + 1)
                if e == 0:
                    pool.wait_ge(rows_done, 1)
                for c in range(3):
                    n = min(P, CAP - c * P)
                    pool.indirect_dma_start(
                        out=yg_d, out_offset=bass.IndirectOffsetOnAxis(ap=row_of[0:n, e, c:c + 1], axis=0),
                        in_=ys[0:n, e % 2, c, :], in_offset=None, bounds_check=TOPK * T - 1, oob_is_err=False
                    ).then_inc(ys_out[e % 2], 16)
            for g in range(2):
                pool.wait_ge(f_vare, g + 1)
                pool.tensor_tensor(out=frstd[:, g * TT // 2:(g + 1) * TT // 2],
                                   in0=fvare[:, g * TT // 2:(g + 1) * TT // 2],
                                   in1=half[:, 0:1].to_broadcast([P, TT // 2]), op=ALU.pow).then_inc(f_rstd, 1)

        @block.tensor
        def _(pe):
            mm = nc.tensor.matmul

            def begin(kind, b=0, n=0):
                u = uno(kind, b, n)
                if u >= GENERAL:
                    pe.wait_ge(*read(*use_list[u - GENERAL]))
                return gB[u % GENERAL]

            def project(kind, b, q):
                g = begin(kind, b, q)
                if kind == "A":
                    pe.wait_ge(x_in[b], 16)
                    pe.wait_ge(wqkv_in, 48)
                    last = mm(g[:, 0:3 * D], xT_sb[:, b, q * P:(q + 1) * P], wqkv[:, :], start=True, stop=True)
                elif kind == "ck":
                    pe.wait_ge(cw_in, 32)
                    pe.wait_ge(c_in[b], 16)
                    last = mm(g[:, 0:L], cwkT[:, :], cT_sb[:, b, :], start=True, stop=True)
                else:
                    for q in range(LT):
                        last = mm(g[:, q * D:(q + 1) * D], cT_sb[:, b, q * P:(q + 1) * P], cwvT[:, :],
                                  start=True, stop=True)
                last.then_inc(g_ready, 1)

            def place(h):
                return h // PAIRS, (h % PAIRS) // 2

            def cross_scores(b, u):
                lt, j = u // PAIRS, u % PAIRS
                n = b * UNITS + u
                if u == 0:
                    pe.wait_ge(ck_in[b % 2], 16 * TERMS * (b // 2 + 1))
                    pe.wait_ge(cq_in[b % 2], 16 * TERMS * (b // 2 + 1))
                if n >= 4:
                    pe.wait_ge(cE_done, n - 3)
                mm(cS[n % 4][:, :], cK[:, b % 2, j, lt * P:(lt + 1) * P],
                   cQ[:, b % 2, j:j + PAIRS + 1:PAIRS, :], start=True, stop=True).then_inc(cs_ready, 1)

            def cross_pv(b, lt, i):
                n = b * LT + lt
                if i == 0:
                    pe.wait_ge(cV_done, 2 * (n + 1))
                    if lt == 0 and b >= 1:
                        pe.wait_ge(o_out, b)
                first = PAIRS * (i // 4) + 4 * (i % 2) + i % 4 // 2
                for h in (first, first + 2):
                    r, c = place(h)
                    last = mm(oC[TILE_COLS * c:TILE_COLS * (c + 1), r * S:(r + 1) * S],
                              cV[:, n % 2, h, :], cE[:, n % 2, h, :],
                              start=(lt == 0 and r == 0 and h % 2 == 0),
                              stop=(lt == LT - 1 and r == 1 and h % 2 == 1), skip_group_check=True)
                if i == PAIRS - 1:
                    last.then_inc(c_pv, 1)

            def norm_step(a, k, b):
                kind = "NC"[a] + k
                if k == "2":
                    g = begin(kind, b)
                    pe.wait_ge(o_out, b + 1)
                    for q in range(QT):
                        for r in range(2):
                            last = nc.tensor.transpose(g[:, (q * 2 + r) * P:(q * 2 + r + 1) * P],
                                                       oSb[:, r * S + q * P:r * S + (q + 1) * P], ident[:, :])
                elif k == "4":
                    g = begin(kind, b)
                    if a == 0:
                        pe.wait_ge(a_in, 16 * (b + 1))
                    else:
                        pe.wait_ge(a_done, b + 1)
                    for q in range(QT):
                        last = nc.tensor.transpose(g[:, q * P:(q + 1) * P], aN[:, a, q, :], ident[:, :])
                elif k == "5":
                    g = begin(kind, b)
                    pe.wait_ge(w_in, 16 * 4)
                    pe.wait_ge(at_done[a], b + 1)
                    for q in range(QT):
                        last = mm(g[:, q * D:(q + 1) * D], aT[:, a, q * P:(q + 1) * P],
                                  (woT, cwoT)[a][:, :], start=True, stop=True)
                elif k == "9":
                    g = begin(kind, b)
                    pe.wait_ge(ln_done[a], QT * (b + 1))
                    for q in range(QT):
                        src = x1[:, b, q, :] if a == 0 else x2[:, b * QT + q, 0:D]
                        last = nc.tensor.transpose(g[:, q * P:(q + 1) * P], src, ident[:, :])
                elif a == 0:
                    g = begin(kind, b)
                    pe.wait_ge(xt_done[0], b + 1)
                    last = mm(g[:, 0:S], cwqT[:, :], x1T[:, :], start=True, stop=True)
                else:
                    g = begin(kind, b)
                    pe.wait_ge(xt_done[1], b + 1)
                    for q in range(QT):
                        last = mm(g[:, q * E:(q + 1) * E], x2T[:, q * P:(q + 1) * P], wg[:, :],
                                  start=True, stop=True)
                last.then_inc(g_ready, 1)

            def ranks(b):
                g = begin("R", b)
                pe.wait_ge(route, b + 1)
                lo, m = QT * b, QT * E
                first = dict(start=True, stop=False, skip_group_check=True)
                last_ = dict(start=False, stop=True, skip_group_check=True)
                mm(g[:, 0:m], lower[:, :], hotb[:, 0, lo:lo + QT, :], **first)
                last = mm(g[:, 0:m], ones[:, :], before[:, 0, lo:lo + QT, :], **last_)
                if b == B - 1:
                    g1 = g[:, m:m + TT * E]
                    mm(g1, lower[:, :], hotb[:, 1, :, :], **first)
                    mm(g1, ones[:, :], before[:, 1, 0:TT, :], start=False, stop=False, skip_group_check=True)
                    last = mm(g1, ones[:, :], before[:, 0, TT:TT + 1, :].to_broadcast([P, TT, E]), **last_)
                last.then_inc(g_ready, 1)

            def work(row):
                for k, b, n in row:
                    if k in ("A", "ck", "cv"):
                        project(k, b, n)
                    elif k == "R":
                        ranks(b)
                    elif k[0] in "NC" and len(k) > 1:
                        norm_step("NC".index(k[0]), k[1:], b)

            pe.wait_ge(cchain, 2)
            work(prologue)
            AHEAD = 2
            for i in range(B):
                for s in range(UNITS):
                    if i == 0 and s == 0:
                        for a in range(AHEAD):
                            cross_scores(0, a)
                    n = i * UNITS + s + AHEAD
                    if n < B * UNITS:
                        cross_scores(n // UNITS, n % UNITS)
                    work(bodies[i][s])
                    n = i * LT + s // PAIRS - 1
                    if n >= 0 and s % PAIRS in PV_AT:
                        for k in range(2):
                            cross_pv(n // LT, n % LT, 2 * PV_AT.index(s % PAIRS) + k)
            for k in range(PAIRS):
                cross_pv(B - 1, LT - 1, k)
            work(last_norm)

            pe.wait_ge(cE_done, B * UNITS)

            def rows_transposed(e):
                pe.wait_ge(xs_in[e], 32)
                if e >= 2:
                    pe.wait_ge(xt_cp, e - 1)
                for c in range(3):
                    n = min(P, CAP - c * P)
                    last = nc.tensor.transpose(cS[e % 2][:, c * P:c * P + n], xs[0:n, e, c, 0:D],
                                               ident[0:n, 0:n])
                last.then_inc(xt_mm, 1)

            def up(e):
                pe.wait_ge(xt_cp, e + 1)
                for f in range(FT):
                    n = e * FT + f
                    if n >= 4:
                        pe.wait_ge(gelu, n - 3)
                    mm([cS[2], cS[3], gB[0], gB[1]][n % 4][:, 0:CAP], fc[:, e, f * P:(f + 1) * P],
                       xsT[:, e * CAP:(e + 1) * CAP], start=True, stop=True).then_inc(h_mm, 1)

            def down(e):
                pe.wait_ge(gelu, FT * (e + 1))
                if e >= 2:
                    pe.wait_ge(y_cp, e - 1)
                for c in range(3):
                    n = min(P, CAP - c * P)
                    for f in range(FT):
                        last = mm([gB[2], oC][e % 2][0:n, c * D:(c + 1) * D], hT[:, e % 3, f, c * P:c * P + n],
                                  pj[:, e, f, :], start=(f == 0), stop=(f == FT - 1))
                last.then_inc(y_mm, 1)

            rows_transposed(0)
            pe.wait_ge(moe_in, 16 * 2 * E)
            pe.wait_ge(rank_read, B)
            rows_transposed(1)
            up(0)
            for e in range(E):
                if e + 2 < E:
                    rows_transposed(e + 2)
                if e + 1 < E:
                    up(e + 1)
                down(e)

        @block.scalar
        def _(act):
            A = nc.scalar.activation

            def copy_proj(kind, b, use):
                n = split_no(kind, b)
                if n >= 2:
                    act.wait_ge(split, 4 * (n - 1))
                await_use(act, *use)
                scale = CROSS_SCALE if kind == "cq" else 1.0
                m = split_len(kind)
                ins = A(proj[:, n % 2, 0:m], bank(*use)[:, 0:m], ACT.Copy, scale=scale)
                ins.then_inc(proj_out, 1)

            def work(row):
                for k, b, n in row:
                    if k == "ck":
                        copy_proj("ck", b, (k, b, 0))
                    elif k == "N10":
                        copy_proj("cq", b, (k, b, 0))
                    elif k == "A":
                        await_use(act, k, b, n)
                        m = b * QT + n
                        if m >= RING:
                            act.wait_ge(pv_done[m % 2], (m - RING) // 2 + 1)
                        A(qkv[:, m % RING, :], bank(k, b, n)[:, 0:3 * D], ACT.Copy).then_inc(qkv_out, 1)
                    elif k == "D":
                        m = b * QT + n
                        act.wait_ge(s_ready, m + 1)
                        if m >= 2:
                            act.wait_ge(f_done, m - 1)
                        A(sP[:, m % 2, :], sS[:, m % 2, :], ACT.Exp, scale=SELF_SCALE).then_inc(p_done, 1)

            work(prologue)
            for i in range(B):
                for s in range(UNITS):
                    n = i * UNITS + s
                    lt, j = s // PAIRS, s % PAIRS
                    g = i * LT + lt
                    act.wait_ge(cm_done, n + 1)
                    if j == 0 and g >= 2:
                        act.wait_ge(c_pv, g - 1)
                        act.wait_ge(crec_done, g - 1)
                    for hf in range(2):
                        ins = A(cE[:, g % 2, hf * PAIRS + j, :], cS[n % 4][:, hf * S:(hf + 1) * S], ACT.Exp,
                                bias=cmx[:, g % 2, hf, j:j + 1],
                                accum_out=csum[:, g % 2, hf * PAIRS + j:hf * PAIRS + j + 1])
                    ins.then_inc(cE_done, 1)
                    work(bodies[i][s])
            act.wait_ge(dz_done, 1)
            A(ez[:, :], dz[:, :], ACT.Exp).then_inc(ex_done, 1)
            for n in range(E * FT):
                e, f = n // FT, n % FT
                act.wait_ge(h_mm, n + 1)
                if e >= 3:
                    act.wait_ge(y_mm, e - 2)
                A(hT[:, e % 3, f, :], [cS[2], cS[3], gB[0], gB[1]][n % 4][:, 0:CAP], ACT.Gelu).then_inc(gelu, 1)

        @block.vector
        def _(dve):
            V = nc.vector
            V.memset(zero[:, :], 0.0).then_inc(zeroed, 1)
            V.memset(cV[:, :, :, :], 0.0).then_inc(pads, 1)
            V.memset(zrow[:, :], 0.0).then_inc(zeroed, 1)
            V.memset(vOne[:, :, :, :, :], 1.0).then_inc(pads, 1)

            steps_done = [0]

            def after(ins):
                steps_done[0] += 1
                ins.then_inc(s_step, 1)
                dve.wait_ge(s_step, steps_done[0])

            def self_step(k, b, q):
                n = b * QT + q
                m = n % 2
                S_ = sS[:, m, :].rearrange("p (a k) -> p a k", a=HEADS)
                if k == "C":
                    dve.wait_ge(qk_done[m], n // 2 + 1)
                    after(V.tensor_reduce(out=sS[:, m, :], in_=prod[:, m, :].rearrange("p (s d) -> p s d", d=HD),
                                          axis=AX.X, op=ALU.add))
                    after(V.tensor_reduce(out=smx[:, m, :], in_=S_, axis=AX.X, op=ALU.max))
                    V.tensor_tensor(out=S_, in0=S_, in1=smx[:, m, :].unsqueeze(2).to_broadcast([P, HEADS, HEADS]),
                                    op=ALU.subtract).then_inc(s_ready, 1)
                elif k == "E":
                    dve.wait_ge(p_done, n + 1)
                    after(V.tensor_reduce(out=ssum[:, m, :], in_=sP[:, m, :].rearrange("p (a k) -> p a k", a=HEADS),
                                          axis=AX.X, op=ALU.add))
                    V.reciprocal(srec[:, m, :], ssum[:, m, :]).then_inc(srec_done, 1)
                elif k == "F":
                    dve.wait_ge(pv_done[m], n // 2 + 1)
                    dve.wait_ge(srec_done, n + 1)
                    if n >= 2:
                        dve.wait_ge(a_st[q], 16 * b)
                    after(V.tensor_reduce(out=sOn[:, m, :], in_=prod[:, m, :].rearrange("p (s k) -> p s k", k=HEADS),
                                          axis=AX.X, op=ALU.add))
                    V.tensor_tensor(out=sO[:, m, :].rearrange("p (a d) -> p a d", d=HD),
                                    in0=sOn[:, m, :].rearrange("p (a d) -> p a d", d=HD),
                                    in1=srec[:, m, :].unsqueeze(2).to_broadcast([P, HEADS, HD]), op=ALU.mult
                                    ).then_inc(f_done, 1)

            count = [0]

            def link(ins):
                count[0] += 1
                ins.then_inc(chain, 1)
                dve.wait_ge(chain, count[0])

            def choose(b):
                tiles = range(QT * b, QT * (b + 1))
                dve.wait_ge(log_done, b + 1)
                for t in tiles:
                    ins = V.max(top[:, t, :], logits[:, t, :])
                link(ins)
                for t in tiles:
                    ins = V.max_index(topi[:, t, :], top[:, t, :], logits[:, t, :])
                link(ins)
                ts = slice(QT * b, QT * (b + 1))
                link(V.tensor_copy(ef[:, :, ts], topi[:, ts, 0:TOPK].rearrange("p t k -> p k t")))
                if b == 0:
                    dve.wait_ge(consts, 2)
                    link(V.memset(before[:, :, 0, :], 0.0))
                for k in range(TOPK):
                    ins = V.tensor_tensor(out=hotb[:, k, ts, :], in0=ef[:, k, ts].unsqueeze(2).to_broadcast([P, QT, E]),
                                          in1=iotaE[:, :].unsqueeze(1).to_broadcast([P, QT, E]), op=ALU.is_equal)
                link(ins)
                for t in tiles:
                    ins = V.tensor_tensor(out=before[:, :, t + 1, :], in0=before[:, :, t, :], in1=hotb[:, :, t, :],
                                          op=ALU.add)
                    if t < tiles[-1]:
                        link(ins)
                ins.then_inc(route, 1)

            def slots(b):
                lo, hi = QT * b, QT * (b + 1) if b < B - 1 else TOPK * TT
                await_use(dve, "R", b)
                V.tensor_tensor(out=rank[:, lo:hi, :],
                                in0=bank("R", b)[:, 0:(hi - lo) * E].rearrange("p (c e) -> p c e", e=E),
                                in1=hotb[:, :, :, :].rearrange("p k t e -> p (k t) e")[:, lo:hi, :], op=ALU.mult
                                ).then_inc(rank_read, 1)
                dve.wait_ge(rank_read, b + 1)
                link(V.tensor_reduce(out=pos[:, lo:hi], in_=rank[:, lo:hi, :], axis=AX.X, op=ALU.add))
                V.tensor_scalar(over[:, lo:hi], pos[:, lo:hi], float(CAP), float(SLOTS), ALU.is_ge, ALU.mult)
                link(V.scalar_tensor_tensor(out=slotf[:, lo:hi], in0=ef[:, :, :].rearrange("p k t -> p (k t)")[:, lo:hi],
                                            scalar=float(CAP), in1=pos[:, lo:hi], op0=ALU.mult, op1=ALU.add))
                V.tensor_tensor(out=slot[:, lo:hi], in0=slotf[:, lo:hi], in1=over[:, lo:hi], op=ALU.add
                                ).then_inc(slot_done, 1)

            def copy_v(b):
                await_use(dve, "cv", b)
                dve.wait_ge(pads, 2)
                V.tensor_copy(vOne[:, b].rearrange("p l h d -> p (l h) d")[:, :, 0:HD],
                              bank("cv", b)[:, 0:LT * D].rearrange("p (lh d) -> p lh d", d=HD)).then_inc(cv_out, 1)

            def sums(g):
                dve.wait_ge(cE_done, PAIRS * (g + 1))
                if g >= 2:
                    dve.wait_ge(cV_done, 2 * (g - 1))
                V.reciprocal(crec[:, g % 2, :], csum[:, g % 2, :]).then_inc(crec_done, 1)

            def evacuate_sums(b):
                dve.wait_ge(c_pv, LT * (b + 1))
                if b >= 1:
                    await_use(dve, "C2", b - 1)
                V.tensor_copy(oSb[:, :], oC[:, :]).then_inc(o_out, 1)

            def norm_step(a, k, b):
                kind = "NC"[a] + k
                await_use(dve, kind, b)
                g = bank(kind, b)
                if k == "2":
                    t = g[:, :].rearrange("p (c x) -> p c x", x=TILE_COLS)[:, :, 0:2 * CV] \
                        .rearrange("p c (s d) -> p c s d", s=2)
                    r = oRec[:, :].rearrange("p (c s) -> p c s", s=2)
                    V.reciprocal(r, t[:, :, :, HD]).then_inc(rec_done, 1)
                    dve.wait_ge(rec_done, b + 1)
                    ins = V.tensor_tensor(
                        out=aN[:, a].rearrange("p q (c s d) -> p (q c) s d", s=2, d=HD), in0=t[:, :, :, 0:HD],
                        in1=r.unsqueeze(3).to_broadcast([P, HEADS, 2, HD]), op=ALU.mult)
                    ins.then_inc(a_done, 1)
                elif k == "4":
                    ins = V.tensor_copy(aT[:, a, :], g[:, 0:S])
                    ins.then_inc(at_done[a], 1)
                elif k == "5":
                    if a == 0:
                        dve.wait_ge(bias_added, b + 1)
                    src = x_sb[:, b] if a == 0 else x1[:, b]
                    ins = V.tensor_tensor(out=pre[:, a].rearrange("p q d -> p (q d)"), in0=g[:, 0:QT * D],
                                          in1=src.rearrange("p q d -> p (q d)"), op=ALU.add)
                    ins.then_inc(pre_done[a], 1)
                elif k == "9":
                    ins = V.tensor_copy((x1T, x2T)[a][:, :], g[:, 0:S])
                    ins.then_inc(xt_done[a], 1)
                else:
                    ins = V.tensor_copy(logits[:, b * QT:(b + 1) * QT, :].rearrange("p q e -> p (q e)"),
                                        g[:, 0:QT * E])
                    ins.then_inc(log_done, 1)

            def layer_norm(a, b):
                dve.wait_ge(pre_done[a], b + 1)
                for q in range(QT):
                    V.bn_stats(stats[:, a, q, :], pre[:, a, q, :]).then_inc(st_done[a], 1)
                for q in range(QT):
                    dve.wait_ge(st_done[a], QT * b + q + 1)
                    V.bn_aggr(mv[:, a, q, :], stats[:, a, q, :]).then_inc(mv_done[a], 1)
                dve.wait_ge(mv_done[a], QT * (b + 1))
                V.tensor_scalar(vare[:, a, :], mv[:, a, :, 1], EPS, None, ALU.add).then_inc(vare_done[a], 1)

            def normalise(a, b):
                dve.wait_ge(rstd_done[a], b + 1)
                for q in range(QT):
                    dst = x1[:, b, q, :] if a == 0 else x2[:, b * QT + q, 0:D]
                    V.tensor_scalar(dst, pre[:, a, q, :], mv[:, a, q, 0:1], rstd[:, a, q:q + 1],
                                    ALU.subtract, ALU.mult).then_inc(ln_done[a], 1)

            def work(row):
                for k, b, n in row:
                    if k == "cv":
                        copy_v(b)
                    elif k == "R":
                        choose(b)
                        slots(b)
                    elif k in "BCEF":
                        if k in "BE":
                            product(dve, V, k, b, n)
                        self_step(k, b, n)
                    elif k[0] in "NC":
                        a = "NC".index(k[0])
                        if k == "N10":
                            continue
                        if k == "N9" and b >= 1:
                            await_use(dve, "N10", b - 1)
                        if k[1:] == "9":
                            normalise(a, b)
                        norm_step(a, k[1:], b)
                        if k[1:] == "5":
                            layer_norm(a, b)

            work(prologue)
            for i in range(B):
                for s in range(UNITS):
                    n = i * UNITS + s
                    lt, j = s // PAIRS, s % PAIRS
                    g = i * LT + lt
                    dve.wait_ge(cs_ready, n + 1)
                    if g >= 2 and j == 0:
                        dve.wait_ge(cE_done, PAIRS * (g - 1))
                    V.tensor_reduce(out=cmx[:, g % 2, :, j], in_=cS[n % 4][:, :].rearrange("p (a t) -> p a t", a=2),
                                    axis=AX.X, op=ALU.max, negate=True).then_inc(cm_done, 1)
                    if s % PAIRS == 1 and g >= 1:
                        sums(g - 1)
                    if s == CROSS_OUT - 1 and i >= 1:
                        evacuate_sums(i - 1)
                    work(bodies[i][s])
            sums(B * LT - 1)
            evacuate_sums(B - 1)
            work(last_norm)

            link(V.tensor_scalar(keep[:, :], pos[:, :], float(CAP), None, ALU.is_lt))
            V.tensor_tensor(out=dz[:, :], in0=top[:, :, 1], in1=top[:, :, 0], op=ALU.subtract).then_inc(dz_done, 1)
            dve.wait_ge(ex_done, 1)
            link(V.tensor_scalar(ez1[:, :], ez[:, :], 1.0, None, ALU.add))
            link(V.reciprocal(w[:, 0, :], ez1[:, :]))
            link(V.tensor_tensor(out=w[:, 1, :], in0=w[:, 0, :], in1=ez[:, :], op=ALU.mult))
            link(V.tensor_tensor(out=w[:, :, :].rearrange("p k t -> p (k t)"),
                                 in0=w[:, :, :].rearrange("p k t -> p (k t)"), in1=keep[:, :], op=ALU.mult))
            def copy_rows(e):
                dve.wait_ge(xt_mm, e + 1)
                V.tensor_copy(xsT[:, e * CAP:(e + 1) * CAP], cS[e % 2][:, 0:CAP]).then_inc(xt_cp, 1)

            copy_rows(0)
            copy_rows(1)
            for e in range(E):
                if e + 2 < E:
                    copy_rows(e + 2)
                if e == 0:
                    for x_ in range(E):
                        dve.wait_ge(xs_in[x_], 32)
                    V.tensor_scalar(row_of[:, :, 0:2], xs[:, :, 0:2, D], float(NONE), None, ALU.add)
                    n = CAP - 2 * P
                    V.tensor_scalar(row_of[0:n, :, 2], xs[0:n, :, 2, D], float(NONE), None, ALU.add
                                    ).then_inc(rows_done, 1)
                dve.wait_ge(y_mm, e + 1)
                if e >= 2:
                    dve.wait_ge(ys_out[e % 2], 16 * 3 * (e // 2))
                V.tensor_copy(ys[:, e % 2, 0:2, :].rearrange("p c d -> p (c d)"), [gB[2], oC][e % 2][:, 0:2 * D])
                V.tensor_copy(ys[0:CAP - 2 * P, e % 2, 2, :], [gB[2], oC][e % 2][0:CAP - 2 * P, 2 * D:3 * D]
                              ).then_inc(y_cp, 1)
            fc_n = [0]

            def flink(ins):
                fc_n[0] += 1
                ins.then_inc(f_chain, 1)
                dve.wait_ge(f_chain, fc_n[0])

            def finish(g):
                dve.wait_ge(f_rstd, g + 1)
                for t in range(g * TT // 2, (g + 1) * TT // 2):
                    V.tensor_scalar(fin[:, t, :], res[:, t, :], fmv[:, t, 0:1], frstd[:, t:t + 1],
                                    ALU.subtract, ALU.mult).then_inc(f_ln, 1)

            for g in range(2):
                tiles = range(g * TT // 2, (g + 1) * TT // 2)
                dve.wait_ge(gath[g], 16 * TOPK)
                for k in range(TOPK):
                    for t in tiles:
                        ins = V.scalar_tensor_tensor(out=res[:, t, :], in0=yg[:, k * TT + t, :],
                                                     scalar=w[:, k, t:t + 1],
                                                     in1=(x2[:, t, 0:D], res[:, t, :])[k],
                                                     op0=ALU.mult, op1=ALU.add)
                    flink(ins)
                for t in tiles:
                    ins = V.bn_stats(fstats[:, t, :], res[:, t, :])
                flink(ins)
                for t in tiles:
                    ins = V.bn_aggr(fmv[:, t, :], fstats[:, t, :])
                flink(ins)
                ts = slice(tiles[0], tiles[-1] + 1)
                V.tensor_scalar(fvare[:, ts], fmv[:, ts, 1], EPS, None, ALU.add).then_inc(f_vare, 1)
                if g >= 1:
                    finish(g - 1)
            finish(1)


def kernel(x, ctx_1024, L0_attn_Wq, L0_attn_Wk, L0_attn_Wv, L0_attn_Wo, L0_attn_bo,
           L0_xattn_Wq, L0_xattn_Wk, L0_xattn_Wv, L0_xattn_Wo, L0_ffn_w_g, L0_ffn_c_fc, L0_ffn_c_proj):
    import numpy as np
    import concourse.bacc as bacc
    from concourse.bass_utils import run_bass_kernel_spmd

    def columns_by_pair(w):
        d = w.shape[1]
        return w.T.reshape(d, 2, PAIRS, d // HEADS).transpose(0, 2, 1, 3).reshape(d, d)

    a = np.asarray
    arrays = {
        "xT": a(x).transpose(2, 0, 1), "x": a(x), "ctxT": a(ctx_1024).transpose(2, 0, 1),
        "attn_wqT": a(L0_attn_Wq).T, "attn_wkT": a(L0_attn_Wk).T,
        "attn_wvT": a(L0_attn_Wv).T, "attn_woT": a(L0_attn_Wo).T, "attn_bo": a(L0_attn_bo),
        "x_wqT": a(L0_xattn_Wq).T, "x_wkT": columns_by_pair(a(L0_xattn_Wk)),
        "x_wvT": a(L0_xattn_Wv).T, "x_woT": a(L0_xattn_Wo).T,
        "w_g": a(L0_ffn_w_g), "c_fc": a(L0_ffn_c_fc), "c_proj": a(L0_ffn_c_proj),
    }
    arrays = {k: np.ascontiguousarray(v) for k, v in arrays.items()}
    nc = bacc.Bacc("TRN2", target_bir_lowering=False, num_devices=1)
    args = [nc.dram_tensor(k, v.shape, mybir.dt.from_np(v.dtype), kind="ExternalInput").ap()
            for k, v in arrays.items()]
    out = nc.dram_tensor("out", a(x).shape, F32, kind="ExternalOutput").ap()
    decoder_layer(nc, *args, out)
    r = run_bass_kernel_spmd(nc, [arrays], core_ids=[0])
    return r.results[0]["out"]
```

```python
from contextlib import ExitStack

import concourse.bass as bass
from concourse import mybir

F32 = mybir.dt.float32
BF16 = mybir.dt.bfloat16
U32 = mybir.dt.uint32
ALU = mybir.AluOpType
ACT = mybir.ActivationFunctionType
AX = mybir.AxisListType

P = 128
HEADS = 16
PAIRS = HEADS // 2
PART_OF_Q = [0, 0, 0, 1, 1, 1, 2, 2]
PART_OF_K = [0, 1, 2, 0, 1, 2, 0, 1]
TERMS = len(PART_OF_Q)
TERM_GROUPS = [(0, 3), (3, 3), (6, 2)]
PARTS = 3
BANK = 512
TILE_COLS = 32
EPS = 1e-5


def decoder_layer(nc, xT, x, ctxT, attn_wqT, attn_wkT, attn_wvT, attn_woT, attn_bo,
                  x_wqT, x_wkT, x_wvT, x_woT, w_g, c_fc, c_proj, out):
    B, S, D = x.shape
    L = ctxT.shape[2]
    E = w_g.shape[1]
    F = c_fc.shape[2]
    HD = D // HEADS
    ROWS = 2 * HD
    QT, LT = S // P, L // P
    T = B * S
    TT = T // P
    TOPK = 2
    CAP = int(TOPK * 1.25 * T / E)
    CAP += CAP % 2
    SLOTS = E * CAP
    FT = F // P
    SELF_SCALE = float(HD) ** -0.5
    CROSS_SCALE = float(D) ** -0.5
    GENERAL = 3
    BANKS = 4
    RING = 4
    PV_AT = [3, 4, 5, 6]
    ZEROS = 4
    NONE = 4 * T
    RW = D + 1
    UNITS = LT * PAIRS
    MAIN = 2 * P
    REST = CAP - MAIN
    assert D == P and REST == P // 2 and E % 2 == 0 and ROWS * TERMS == P and S == 256 and FT * P == F
    CV = HD + 1

    SECOND_HALF = [(0, "sm", 0), (0, "pv", 0), (1, "sm", 1), (4, "o", 0), (5, "pv", 1), (7, "o", 1),
                   (7, "pv", 2), (7, "pv", 3), (10, "o", 2), (10, "o", 3), (15, "N4", 0), (17, "N5", 0),
                   (18, "N9", 0), (20, "N10", 0)]
    FIRST_HALF = [(9, "A", 0), (10, "qk", 0), (12, "A", 1), (12, "qk", 1), (12, "qk", 2), (15, "s", 0),
                  (15, "s", 1), (19, "s", 2), (19, "qk", 3), (21, "p", 0), (22, "mx", 0), (24, "s", 3),
                  (25, "mx", 1), (25, "ck", 0), (26, "p", 1), (27, "cv", 0)]
    LATER = [(0, 0), (4, 0), (0, 0), (0, -1)]
    C_TAIL = [(5, "C1"), (8, "C2"), (9, "C4"), (12, "C5"), (14, "C9"), (18, "C10"), (21, "R")]
    WARM = 10
    LAG = 2
    GROUPS = 4
    GT = TT // GROUPS
    COPIES_BY_ACT = ("C1", "C10", "C4", "C9", "N4", "N9")
    K_READ = 1
    LEAD_PE = 1
    AHEAD = 2

    PRODUCT_ON_DVE = {("qk", 0, 0), ("qk", 0, 1), ("pv", 0, 0), ("pv", 0, 3)}
    prologue = [
        ("qk", 0, 0), ("qk", 0, 1), ("A", 0, 0), ("qk", 0, 2), ("s", 0, 0), ("qk", 0, 3), ("A", 0, 1),
        ("s", 0, 1), ("ck", 0, 0), ("p", 0, 0), ("mx", 0, 0), ("p", 0, 1), ("cv", 0, 0), ("sm", 0, 0),
        ("in", 1, 0), ("s", 0, 2), ("pv", 0, 0), ("pv", 0, 1), ("s", 0, 3), ("pv", 0, 2), ("A", 1, 0),
        ("o", 0, 0), ("mx", 0, 1), ("qk", 1, 0), ("sm", 0, 1), ("o", 0, 1), ("qk", 1, 1), ("A", 1, 1),
        ("pv", 0, 3), ("o", 0, 2), ("o", 0, 3), ("s", 1, 0), ("s", 1, 1), ("N4", 0, 0), ("qk", 1, 2),
        ("mx", 1, 0), ("N5", 0, 0), ("N9", 0, 0), ("N10", 0, 0), ("p", 1, 0), ("s", 1, 2), ("in", 2, 0),
        ("s", 1, 3), ("mx", 1, 1), ("qk", 1, 3), ("cv", 1, 0), ("ck", 1, 0), ("p", 1, 1),
    ]

    rows = [[] for _ in range(B * UNITS)]
    for b in range(B - 1):
        for s, k in C_TAIL:
            rows[UNITS * (b + 1) + s].append((k, b, 0))
    for b in range(1, B):
        for s, k, q in SECOND_HALF:
            rows[UNITS * (b - 1) + s + LATER[b][1]].append((k, b, q))
    for b in range(2, B):
        for s, k, q in FIRST_HALF:
            rows[UNITS * (b - 2) + s + LATER[b][0]].append((k, b, q))
    for b in range(2, B):
        rows[UNITS * (b - 1) + K_READ].append(("kr", b, 0))
    for b in range(3, B):
        rows[UNITS * (b - 3) + 21].append(("in", b, 0))
    for n in range(2 * ZEROS):
        rows[4 * n + 3].append(("z", n, 0))
    for n in range(2 * E):
        rows[UNITS + 4 * n + 3].append(("w", n, 0))

    def rows_at(n, lead=0):
        first, last = n + lead, n + lead + 1
        if n == 0:
            first = 0
        if n == B * UNITS - 1:
            last = B * UNITS
        return [x for row in rows[max(first, 0):max(last, 0)] for x in row]

    last_norm = [(k, B - 1, 0) for _, k in C_TAIL]
    steps = prologue + [x for row in rows for x in row] + last_norm

    def count_of(x):
        return (x[0], x[2] % 2) if x[0] == "pv" else x[0]

    for kind in {count_of(x) for x in steps}:
        assert [x for x in steps if count_of(x) == kind] == sorted(x for x in steps if count_of(x) == kind), kind
    use_list = [x for x in steps if x[0] in ("A", "ck", "cv", "R") or (x[0][0] in "NC" and x[0] != "C1")]
    use_no = {x: n for n, x in enumerate(use_list)}
    split_order = [{"ck": "ck", "N10": "cq"}[k] + str(b) for k, b, _ in steps if k in ("ck", "N10")]

    ctx = ExitStack()
    with ctx:
        def sb(name, shape, dt=F32):
            return ctx.enter_context(nc.sbuf_tensor(name, shape, dt))

        def sem(name):
            return ctx.enter_context(nc.semaphore(name))

        wqkv = sb("wqkv", [P, 3 * D])
        woT = sb("woT", [P, D])
        cwqT = sb("cwqT", [P, D]); cwkT = sb("cwkT", [P, D]); cwvT = sb("cwvT", [P, D]); cwoT = sb("cwoT", [P, D])
        bo = sb("bo", [P, D])
        wg = sb("wg", [P, E])
        xT_sb = sb("xT_sb", [P, B, S])
        cT_sb = sb("cT_sb", [P, B, L])
        x_sb = sb("x_sb", [P, B, QT, D])
        fc = sb("fc", [P, E, F])
        proj = sb("proj", [P, 2, L])
        rest = sb("rest", [P, 2, L])
        parts = sb("parts", [P, 2, PARTS, L], BF16)
        zero = sb("zero", [96, 6 * HD * PAIRS * S // 96], BF16)
        zrow = sb("zrow", [P, SLOTS * RW // P // ZEROS])
        qkv = sb("qkv", [P, RING, 3 * D])
        prod = sb("prod", [P, 2, HEADS * HEADS * HD])
        sS = sb("sS", [P, 2, HEADS * HEADS])
        sP = sb("sP", [P, 2, HEADS * HEADS])
        smx = sb("smx", [P, 2, HEADS])
        ssum = sb("ssum", [P, 2, HEADS])
        srec = sb("srec", [P, 2, HEADS])
        sOn = sb("sOn", [P, 2, D])
        sO = sb("sO", [P, 2, D])
        cQ = sb("cQ", [P, 2, HEADS, S], BF16)
        cK = sb("cK", [P, 2, PAIRS, L], BF16)
        vOne = sb("vOne", [P, B, LT, HEADS, CV])
        cV = sb("cV", [P, 2, HEADS, TILE_COLS])
        cE = sb("cE", [P, 2, HEADS, S])
        cmx = sb("cmx", [P, 2, 2, PAIRS])
        csum = sb("csum", [P, 2, HEADS])
        crec = sb("crec", [P, 2, HEADS])
        oSb = sb("oSb", [P, BANK])
        oRec = sb("oRec", [P, 2 * HEADS])   
        pj = sb("pj", [P, E, FT, D])
        aN = sb("aN", [P, 2, QT, D])
        aT = sb("aT", [P, 2, S])
        pre = sb("pre", [P, 2, QT, D])
        stats = sb("stats", [P, 2, QT, 6])
        mv = sb("mv", [P, 2, QT, 2])
        vare = sb("vare", [P, 2, QT])
        half = sb("half", [P, 2])
        rstd = sb("rstd", [P, 2, QT])
        x1 = sb("x1", [P, B, QT, D])
        x1T = sb("x1T", [P, S])
        x2 = sb("x2", [P, TT, RW])
        x2T = sb("x2T", [P, S])
        ident = sb("ident", [P, P])
        logits = sb("logits", [P, TT, E])
        top = sb("top", [P, TT, 8])
        topi = sb("topi", [P, TT, 8], U32)
        ef = sb("ef", [P, TOPK, TT])
        iotaE = sb("iotaE", [P, E])
        hotb = sb("hotb", [P, TOPK, TT, E], BF16)
        before = sb("before", [P, TOPK, TT + 1, E], BF16)
        lower = sb("lower", [P, P], BF16)
        ones = sb("ones", [P, P], BF16)
        rank = sb("rank", [P, 3, QT, E])
        place_of = sb("place_of", [P, TT, 3])
        base_of = sb("base_of", [P, TOPK, TT])
        over = sb("over", [P, TOPK, QT])
        slotf = sb("slotf", [P, TOPK, QT])
        slot = sb("slot", [P, TOPK, TT], U32)
        firsts = sb("firsts", [P, E])
        queue = sb("queue", [P, TT, E])
        behind = sb("behind", [P, TT])
        keep = sb("keep", [P, TOPK, TT])
        iotaS = sb("iotaS", [P, 3])
        second = sb("second", [P, E // 2, 5])
        row_of = sb("row_of", [P, E // 2, 5], U32)
        dz = sb("dz", [P, TT])
        ez = sb("ez", [P, TT])
        ez1 = sb("ez1", [P, TT])
        w = sb("w", [P, TOPK, TT])
        cE_flat = cE[:, :, :, :].rearrange("p a h t -> p (a h t)")
        XS = 5 * E // 2 * RW
        xs = cE_flat[:, 0:XS].rearrange("p (e c d) -> p e c d", e=E // 2, d=RW)
        xsT = cE_flat[:, XS:XS + SLOTS]
        yg = cE_flat[:, XS + SLOTS:XS + SLOTS + TOPK * TT * D].rearrange("p (c d) -> p c d", d=D)
        hT = prod[:, :, :].rearrange("p a x -> p (a x)")[:, 0:3 * FT * CAP].rearrange(
            "p (a f c) -> p a f c", a=3, f=FT)
        assert XS + SLOTS + TOPK * TT * D <= 2 * HEADS * S and 3 * FT * CAP <= 2 * HEADS * HEADS * HD
        ys = sb("ys", [P, 2, 3, D])
        res = xT_sb[:, :, :].rearrange("p b t -> p (b t)").rearrange("p (t d) -> p t d", d=D)
        fin = cT_sb[:, :, :].rearrange("p b t -> p (b t)")[:, 0:T].rearrange("p (t d) -> p t d", d=D)
        fstats = sb("fstats", [P, TT, 6])
        fmv = sb("fmv", [P, TT, 2])
        fvare = sb("fvare", [P, TT])
        frstd = sb("frstd", [P, TT])
        fneg = sb("fneg", [P, TT])
        fshift = sb("fshift", [P, TT])

        cS = [ctx.enter_context(nc.psum_tensor(f"cS{i}", [P, BANK], F32)) for i in range(BANKS)]
        gB = [ctx.enter_context(nc.psum_tensor(f"gB{i}", [P, BANK], F32)) for i in range(GENERAL)]
        oC = ctx.enter_context(nc.psum_tensor("oC", [P, BANK], F32))

        h_banks, y_banks = [cS[2], cS[3], gB[0], gB[1]], [(cS + gB)[-1 if GENERAL > 2 else 4], oC]

        q_scr = nc.dram_tensor("q_scr", (2, PARTS, 2, 2, HD * PAIRS, S), BF16, kind="Internal").ap()
        ck_scr = nc.dram_tensor("ck_scr", (B, PARTS, P, L), BF16, kind="Internal").ap()
        a_scr = nc.dram_tensor("a_scr", (B, HEADS, S, HD), F32, kind="Internal").ap()
        xs_d = nc.dram_tensor("xs_d", (SLOTS, RW), F32, kind="Internal").ap()
        yg_d = nc.dram_tensor("yg_d", (TOPK * T, D), F32, kind="Internal").ap()

        wqkv_in = sem("wqkv_in")
        w_in = sem("w_in")
        x_in = [sem(f"x_in{b}") for b in range(B)]
        c_in = [sem(f"c_in{b}") for b in range(B)]
        res_in = [sem(f"res_in{b}") for b in range(B)]
        cw_in = sem("cw_in")
        moe_in = sem("moe_in")
        zeroed = sem("zeroed")
        consts = sem("consts")
        cchain = sem("cchain")
        bias_added = sem("bias_added")
        pads = sem("pads")
        pad_dma = sem("pad_dma")
        xs_zero = sem("xs_zero")
        g_ready = sem("g_ready")
        proj_out = sem("proj_out")
        split = sem("split")
        parts_out = [sem("parts_out0"), sem("parts_out1")]
        ck_in = [sem("ck_in0"), sem("ck_in1")]
        cq_in = [sem("cq_in0"), sem("cq_in1")]
        cv_out = sem("cv_out")
        qkv_out = sem("qkv_out")
        qk_done = [sem("qk_done0"), sem("qk_done1")]
        s_step = sem("s_step")
        s_sum = sem("s_sum")
        o_sum = sem("o_sum")
        s_ready = sem("s_ready")
        p_done = sem("p_done")
        pv_done = [[sem(f"pv_done{m}{h}") for h in range(2)] for m in range(2)]
        srec_done = sem("srec_done")
        o_done = sem("o_done")
        a_st = [sem("a_st0"), sem("a_st1")]
        a_in = sem("a_in")
        c_pv = sem("c_pv")
        cs_ready = sem("cs_ready")
        cm_done = sem("cm_done")
        cE_done = sem("cE_done")
        crec_done = sem("crec_done")
        cV_done = sem("cV_done")
        o_out = sem("o_out")
        rec_done = sem("rec_done")
        a_done = sem("a_done")
        at_done = [sem("at_doneS"), sem("at_doneC")]
        pre_done = [sem("pre_doneS"), sem("pre_doneC")]
        st_done = [sem("st_doneS"), sem("st_doneC")]
        mv_done = [sem("mv_doneS"), sem("mv_doneC")]
        vare_done = [sem("vare_doneS"), sem("vare_doneC")]
        rstd_done = [sem("rstd_doneS"), sem("rstd_doneC")]
        ln_done = [sem("ln_doneS"), sem("ln_doneC")]
        xt_done = [sem("xt_doneS"), sem("xt_doneC")]
        log_done = sem("log_done")
        chain = sem("chain")
        route = sem("route")
        w_done = sem("w_done")
        dz_done = sem("dz_done")
        ex_done = sem("ex_done")
        rank_read = sem("rank_read")
        slot_done = sem("slot_done")
        scat = [sem(f"scat{b}") for b in range(B)]
        xs_in = [sem(f"xs_in{e}") for e in range(E // 2)]
        xt_mm = sem("xt_mm"); xt_cp = sem("xt_cp")
        rows_done = sem("rows_done")
        h_mm = sem("h_mm"); gelu = sem("gelu")
        y_mm = sem("y_mm"); y_cp = sem("y_cp")
        ys_out = [sem("ys_out0"), sem("ys_out1")]
        gath = [sem(f"gath{g}") for g in range(GROUPS)]
        f_weighed = sem("f_weighed")
        f_first = sem("f_first")
        f_chain = sem("f_chain")
        f_vare = sem("f_vare")
        f_rstd = sem("f_rstd")
        f_shift = sem("f_shift")
        f_ln = sem("f_ln")
        stored = sem("stored")
        block = ctx.enter_context(nc.Block())

        def uno(kind, b=0, n=0):
            return use_no[(kind, b, n)]

        def bank(kind, b=0, n=0):
            return gB[uno(kind, b, n) % GENERAL]

        def await_use(eng, kind, b=0, n=0):
            eng.wait_ge(g_ready, uno(kind, b, n) + 1)

        def read(kind, b, n):
            if kind == "A":
                return qkv_out, b * QT + n + 1
            if kind == "cv":
                return cv_out, b + 1
            if kind == "ck":
                return proj_out, split_no("ck", b) + 1
            if kind == "N10":
                return proj_out, split_no("cq", b) + 1
            return {"C2": a_done, "N4": at_done[0], "C4": at_done[1], "N5": pre_done[0], "C5": pre_done[1],
                    "N9": xt_done[0], "C9": xt_done[1], "C10": log_done, "R": rank_read}[kind], b + 1

        def split_no(kind, b):
            return split_order.index(kind + str(b))

        def split_len(kind):
            return L if kind == "ck" else S

        def y_tiles(e):
            return 5 * (e // 2) + (5 if e % 2 else 2)

        Q_READS, K_READS = 2 * len(TERM_GROUPS), len(TERM_GROUPS)
        parts_count = {}
        cnt = [0, 0]
        for n, name in enumerate(split_order):
            cnt[n % 2] += 16 * (2 if name[:2] == "cq" else 1)
            parts_count[name] = cnt[n % 2]

        def copy_out(eng, k, b):
            if (eng is nc.scalar) != (k in COPIES_BY_ACT):
                return

            def copy(dst, src):
                if eng is nc.scalar:
                    return nc.scalar.activation(dst, src, ACT.Copy)
                return nc.vector.tensor_copy(dst, src)

            if k == "C1":
                eng.wait_ge(c_pv, LT * (b + 1))
                if b >= 1:
                    await_use(eng, "C2", b - 1)
                copy(oSb[:, :], oC[:, :]).then_inc(o_out, 1)
                return
            await_use(eng, k, b)
            g = bank(k, b)
            if k == "cv":
                eng.wait_ge(pads, 2)
                copy(vOne[:, b].rearrange("p l h d -> p (l h) d")[:, :, 0:HD],
                     g[:, 0:LT * D].rearrange("p (lh d) -> p lh d", d=HD)).then_inc(cv_out, 1)
            elif k in ("N4", "C4"):
                a = "NC".index(k[0])
                copy(aT[:, a, :], g[:, 0:S]).then_inc(at_done[a], 1)
            elif k in ("N9", "C9"):
                a = "NC".index(k[0])
                if k == "N9" and b >= 1:
                    await_use(eng, "N10", b - 1)
                copy((x1T, x2T)[a][:, :], g[:, 0:S]).then_inc(xt_done[a], 1)
            elif k == "C10":
                copy(logits[:, b * QT:(b + 1) * QT, :].rearrange("p q e -> p (q e)"), g[:, 0:QT * E]
                     ).then_inc(log_done, 1)

        def product(eng, api, k, b, x):
            if (eng is nc.vector) != ((k, b, x) in PRODUCT_ON_DVE):
                return
            q, h = x // 2, x % 2
            n = b * QT + q
            HH = HEADS // 2
            out_ = prod[:, n % 2, h * HH * HEADS * HD:(h + 1) * HH * HEADS * HD]
            if k == "qk":
                eng.wait_ge(qkv_out, n + 1)
                if n >= 2:
                    eng.wait_ge(o_done, n - 1)
                api.tensor_tensor(
                    out=out_.rearrange("p (a k d) -> p a k d", a=HH, d=HD),
                    in0=qkv[:, n % RING, h * D // 2:(h + 1) * D // 2].rearrange("p (a d) -> p a d", d=HD).unsqueeze(2)
                    .to_broadcast([P, HH, HEADS, HD]),
                    in1=qkv[:, n % RING, D:2 * D].rearrange("p (k d) -> p k d", d=HD).unsqueeze(1)
                    .to_broadcast([P, HH, HEADS, HD]), op=ALU.mult).then_inc(qk_done[n % 2], 1)
            else:
                eng.wait_ge(p_done, n + 1)
                api.tensor_tensor(
                    out=out_.rearrange("p (a d k) -> p a d k", a=HH, d=HD),
                    in0=sP[:, n % 2, h * HH * HEADS:(h + 1) * HH * HEADS].rearrange("p (a k) -> p a k", a=HH)
                    .unsqueeze(2).to_broadcast([P, HH, HD, HEADS]),
                    in1=qkv[:, n % RING, 2 * D:3 * D].rearrange("p (k d) -> p d k", d=HD).unsqueeze(1)
                    .to_broadcast([P, HH, HD, HEADS]), op=ALU.mult).then_inc(pv_done[n % 2][h], 1)

        @block.sync
        def _(sp):
            sp.dma_start(xT_sb[:, 0, :], xT[:, 0, :]).then_inc(x_in[0], 16)
            for n, src in enumerate((attn_wqT, attn_wkT, attn_wvT)):
                sp.dma_start(wqkv[:, n * D:(n + 1) * D], src).then_inc(wqkv_in, 16)
            sp.dma_start(xT_sb[:, 1, :], xT[:, 1, :]).then_inc(x_in[1], 16)
            sp.dma_start(cwkT[:, :], x_wkT).then_inc(cw_in, 16)
            sp.dma_start(cwvT[:, :], x_wvT).then_inc(cw_in, 16)
            sp.dma_start(cT_sb[:, 0, :], ctxT[:, 0, :]).then_inc(c_in[0], 16)
            sp.dma_start(bo[:, :], attn_bo.partition_broadcast(P)).then_inc(res_in[0], 16)
            sp.dma_start(x_sb[:, 0, :, :], x[0].rearrange("(q p) d -> p q d", p=P)).then_inc(res_in[0], 16)
            for dst, src in ((woT, attn_woT), (cwqT, x_wqT), (cwoT, x_woT), (wg, w_g)):
                sp.dma_start(dst[:, :], src).then_inc(w_in, 16)
            sp.wait_ge(zeroed, 1)
            for hf in range(2):
                sp.dma_start(q_scr[:, :, hf, 1 - hf, :, :].rearrange("b p x t -> (b p) (x t)"), zero[:, :]
                             ).then_inc(pad_dma, 16)

            def write_parts(kind, b):
                n = split_no(kind, b)
                sp.wait_ge(split, 4 * (n + 1))
                if kind == "cq":
                    if b >= 2:
                        sp.wait_ge(cq_in[b % 2], 16 * Q_READS * (b // 2))
                    for hf in range(2):
                        sp.dma_start(q_scr[b % 2, :, hf, hf, :, :].rearrange("p x t -> x p t"),
                                     parts[hf * 64:(hf + 1) * 64, n % 2, :, 0:S]).then_inc(parts_out[n % 2], 16)
                else:
                    sp.dma_start(ck_scr[b].rearrange("p x t -> x p t"), parts[:, n % 2, :, :]
                                 ).then_inc(parts_out[n % 2], 16)

            def read_stack(kind, b):
                n = split_no(kind, b)
                sp.wait_ge(parts_out[n % 2], parts_count[kind + str(b)])
                if b == 0 and kind == "cq":
                    sp.wait_ge(pad_dma, 32)
                if b >= 2:
                    sp.wait_ge(cs_ready, UNITS * (b - 1))
                for first, count in TERM_GROUPS:
                    rows = slice(ROWS * first, ROWS * (first + count))
                    if kind == "cq":
                        for hf in range(2):
                            src = q_scr[b % 2, PART_OF_Q[first], hf].rearrange("s (d j) t -> (s d) (j t)", j=PAIRS)
                            sp.dma_start(cQ[rows, b % 2, hf * PAIRS:(hf + 1) * PAIRS, :],
                                         src.unsqueeze(0).to_broadcast([count, ROWS, PAIRS * S])
                                         ).then_inc(cq_in[b % 2], 16)
                    else:
                        sp.dma_start(cK[rows, b % 2, :, :],
                                     ck_scr[b, 0:count].rearrange("p (r j) t -> (p r) (j t)", j=PAIRS)
                                     ).then_inc(ck_in[b % 2], 16)

            def work(row):
                for k, b, q in row:
                    if k == "in":
                        if b >= 2:
                            sp.dma_start(xT_sb[:, b, :], xT[:, b, :]).then_inc(x_in[b], 16)
                        sp.dma_start(cT_sb[:, b, :], ctxT[:, b, :]).then_inc(c_in[b], 16)
                        sp.dma_start(x_sb[:, b, :, :], x[b].rearrange("(q p) d -> p q d", p=P)).then_inc(res_in[b], 16)
                    elif k == "z":
                        if b == 0:
                            sp.wait_ge(zeroed, 2)
                        n = b % ZEROS
                        dst = (xs_d if b < ZEROS else yg_d).rearrange("(z p r) d -> z p (r d)", z=ZEROS, p=P)[n]
                        sp.dma_start(dst, zrow[:, 0:dst.shape[1]]).then_inc(xs_zero, 16)
                    elif k == "w":
                        e = b // 2
                        if b % 2 == 0:
                            sp.dma_start(fc[:, e, :], c_fc[e]).then_inc(moe_in, 16)
                        else:
                            sp.dma_start(pj[:, e, :, :], c_proj[e].rearrange("(a f) d -> f a d", f=P)
                                         ).then_inc(moe_in, 16)
                    elif k == "ck":
                        write_parts("ck", b)
                        if b < 2:
                            read_stack("ck", b)
                    elif k == "kr":
                        read_stack("ck", b)
                    elif k == "N10":
                        write_parts("cq", b)
                        read_stack("cq", b)
                    elif k == "o" and q % 2:
                        q //= 2
                        n = b * QT + q
                        sp.wait_ge(o_done, n + 1)
                        sp.dma_start(a_scr[b, :, q * P:(q + 1) * P, :].rearrange("h s d -> s h d"),
                                     sO[:, n % 2, :].rearrange("p (h d) -> p h d", d=HD)).then_inc(a_st[q], 16)
                    elif k == "N4":
                        for q in range(QT):
                            sp.wait_ge(a_st[q], 16 * (b + 1))
                        if b >= 1:
                            await_use(sp, "N4", b - 1)
                        sp.dma_start(aN[:, 0, :, :], a_scr[b].rearrange("h (r x) d -> (h r) (x d)", x=HEADS)
                                     .rearrange("(q p) c -> p q c", p=P)).then_inc(a_in, 16)

            work(prologue)
            for row in rows:
                work(row)
            for b in range(B):
                sp.wait_ge(scat[b], 16 * TOPK * QT)
            for e in range(0, E, 2):
                for s in range(2):
                    first = (e + s) * CAP
                    sp.dma_start(xs[:, e // 2, 2 * s:2 * s + 2, :],
                                 xs_d[first:first + MAIN, :].rearrange("(c p) d -> p c d", p=P)
                                 ).then_inc(xs_in[e // 2], 16)
                    if s == 0:
                        rest_ = xs_d[e * CAP:(e + 2) * CAP, :].rearrange("(e r) d -> e r d", e=2)[:, MAIN:CAP, :]
                        sp.dma_start(xs[:, e // 2, 4, :], rest_).then_inc(xs_in[e // 2], 16)
            sp.wait_ge(ys_out[0], 16 * 2 * (E // 2))
            sp.wait_ge(ys_out[1], 16 * 3 * (E // 2))
            for g in range(GROUPS):
                for k in range(TOPK):
                    c = k * TT + g * GT
                    sp.dma_start(yg[:, c:c + GT, :], yg_d[c * P:(c + GT) * P, :]
                                 .rearrange("(t p) d -> p t d", p=P)).then_inc(gath[g], 16)
            for g in range(GROUPS):
                sp.wait_ge(f_ln, g + 1)
                sp.dma_start(out.rearrange("b (q p) d -> p (b q) d", p=P)[:, GT * g:GT * (g + 1), :],
                             fin[:, GT * g:GT * (g + 1), :]).then_inc(stored, 16)
            sp.wait_ge(stored, 16 * GROUPS)

        @block.gpsimd
        def _(pool):
            pool.memset(half[:, :], -0.5).then_inc(consts, 1)
            made = [0]

            def step(ins):
                made[0] += 1
                ins.then_inc(cchain, 1)
                pool.wait_ge(cchain, made[0])

            step(pool.memset(ident[:, :], 0.0))
            step(pool.affine_select(out=ident[:, :], in_=ident[:, :], compare_op=ALU.not_equal, fill=1.0,
                                    base=0, pattern=[[-1, P]], channel_multiplier=1))
            def split_parts(kind, b):
                n = split_no(kind, b)
                m = split_len(kind)
                src, r, pt = proj[:, n % 2, 0:m], rest[:, n % 2, 0:m], parts[:, n % 2]
                pool.wait_ge(proj_out, n + 1)
                if n >= 2:
                    pool.wait_ge(parts_out[n % 2], parts_count[split_order[n - 2]])
                pool.tensor_scalar(pt[:, 0, 0:m], src, 1.0, 1.0, ALU.mult, ALU.mult).then_inc(split, 1)
                pool.wait_ge(split, 4 * n + 1)
                pool.tensor_tensor(out=r, in0=src, in1=pt[:, 0, 0:m], op=ALU.subtract).then_inc(split, 1)
                pool.wait_ge(split, 4 * n + 2)
                pool.tensor_scalar(pt[:, 1, 0:m], r, 1.0, 1.0, ALU.mult, ALU.mult).then_inc(split, 1)
                pool.wait_ge(split, 4 * n + 3)
                pool.tensor_tensor(out=pt[:, 2, 0:m], in0=r, in1=pt[:, 1, 0:m], op=ALU.subtract).then_inc(split, 1)

            def power(a, b):
                pool.wait_ge(vare_done[a], b + 1)
                if b >= 1:
                    pool.wait_ge(ln_done[a], QT * b)
                pool.tensor_tensor(out=rstd[:, a, :], in0=vare[:, a, :], in1=half[:, 0:QT], op=ALU.pow
                                   ).then_inc(rstd_done[a], 1)

            def scale_v(b, lt):
                n = b * LT + lt
                pool.wait_ge(crec_done, n + 1)
                pool.wait_ge(cv_out, b + 1)
                if n >= 2:
                    pool.wait_ge(c_pv, n - 1)
                for s in range(2):
                    v = vOne[:, b, lt].rearrange("p (c s) d -> p c s d", s=2)[:, :, s, :]
                    o = cV[:, n % 2].rearrange("p (c s) d -> p c s d", s=2)[:, :, s, s * CV:(s + 1) * CV]
                    r = crec[:, n % 2].rearrange("p (c s) -> p c s", s=2)[:, :, s:s + 1]
                    pool.tensor_tensor(out=o, in0=v, in1=r.to_broadcast([P, HEADS // 2, CV]), op=ALU.mult
                                       ).then_inc(cV_done, 1)

            def scatter(b):
                pool.wait_ge(slot_done, b + 1)
                if b == 0:
                    pool.wait_ge(xs_zero, 16 * 2 * ZEROS)
                    pool.wait_ge(consts, 2)
                else:
                    pool.wait_ge(scat[b - 1], 16 * TOPK * QT)
                for k in range(TOPK):
                    for t in range(QT * b, QT * (b + 1)):
                        pool.indirect_dma_start(
                            out=xs_d, out_offset=bass.IndirectOffsetOnAxis(ap=slot[:, k, t:t + 1], axis=0),
                            in_=x2[:, t, :], in_offset=None, bounds_check=SLOTS - 1, oob_is_err=False
                        ).then_inc(scat[b], 16)

            def work(row):
                for k, b, n in row:
                    if k == "ck":
                        split_parts("ck", b)
                    elif k == "R":
                        scatter(b)
                    elif k in ("qk", "pv"):
                        product(pool, nc.gpsimd, k, b, n)
                    elif k == "o" and n == 0:
                        pool.wait_ge(res_in[0], 32)
                        if b >= 1:
                            pool.wait_ge(res_in[b], 16)
                        pool.tensor_tensor(out=x_sb[:, b, :, :], in0=x_sb[:, b, :, :],
                                           in1=bo[:, :].unsqueeze(1).to_broadcast([P, QT, D]), op=ALU.add
                                           ).then_inc(bias_added, 1)
                    elif k == "N5":
                        power(0, b)
                    elif k == "C5":
                        power(1, b)
                    elif k == "N10":
                        split_parts("cq", b)

            pool.wait_ge(pads, 2)
            work(prologue)
            step(pool.memset(ones[:, :], 1.0))
            step(pool.affine_select(out=lower[:, :], in_=ones[:, :], compare_op=ALU.is_gt, fill=0.0,
                                    base=0, pattern=[[1, P]], channel_multiplier=-1))
            step(pool.iota(iotaE[:, :], pattern=[[1, E]], base=0, channel_multiplier=0,
                           allow_small_or_imprecise_dtypes=True))
            step(pool.iota(iotaS[:, :], pattern=[[P, 3]], base=0, channel_multiplier=1,
                           allow_small_or_imprecise_dtypes=True))
            pool.iota(x2[:, :, D:D + 1], pattern=[[P, TT], [0, 1]], base=-NONE, channel_multiplier=1,
                      allow_small_or_imprecise_dtypes=True).then_inc(consts, 1)
            for i in range(B):
                for s in range(UNITS):
                    if s % PAIRS == 1 and (i or s >= PAIRS):
                        n = i * LT + s // PAIRS - 1
                        scale_v(n // LT, n % LT)
                    work(rows_at(i * UNITS + s))
            scale_v(B - 1, LT - 1)
            work(last_norm)
            for e in range(E):
                if e == 0:
                    pool.wait_ge(rows_done, 1)
                s = e % 2
                for c, col in ((0, 2 * s), (1, 2 * s + 1), (2, 4))[0:2 + s]:
                    pool.wait_ge(y_cp, y_tiles(e) - (2 + s) + c + 1)
                    pool.indirect_dma_start(
                        out=yg_d, out_offset=bass.IndirectOffsetOnAxis(ap=row_of[:, e // 2, col:col + 1], axis=0),
                        in_=ys[:, s, c, :], in_offset=None, bounds_check=TOPK * T - 1, oob_is_err=False
                    ).then_inc(ys_out[s], 16)
            for g in range(GROUPS + LAG):
                if g < GROUPS:
                    ts = slice(g * GT, (g + 1) * GT)
                    pool.wait_ge(f_weighed, g + 1)
                    pool.tensor_tensor(out=res[:, ts, :], in0=yg[:, ts, :], in1=x2[:, ts, 0:D], op=ALU.add
                                       ).then_inc(f_first, 1)
                if g >= LAG:
                    ts = slice((g - LAG) * GT, (g - LAG + 1) * GT)
                    pool.wait_ge(f_vare, g - LAG + 1)
                    pool.tensor_tensor(out=frstd[:, ts], in0=fvare[:, ts], in1=half[:, 0:GT], op=ALU.pow
                                       ).then_inc(f_rstd, 1)
                    pool.wait_ge(f_rstd, g - LAG + 1)
                    pool.tensor_tensor(out=fshift[:, ts], in0=fneg[:, ts], in1=frstd[:, ts], op=ALU.mult
                                       ).then_inc(f_shift, 1)

        @block.tensor
        def _(pe):
            mm = nc.tensor.matmul

            def begin(kind, b=0, n=0):
                u = uno(kind, b, n)
                if u >= GENERAL:
                    pe.wait_ge(*read(*use_list[u - GENERAL]))
                return gB[u % GENERAL]

            def project(kind, b, q):
                g = begin(kind, b, q)
                if kind == "A":
                    pe.wait_ge(x_in[b], 16)
                    pe.wait_ge(wqkv_in, 48)
                    last = mm(g[:, 0:3 * D], xT_sb[:, b, q * P:(q + 1) * P], wqkv[:, :], start=True, stop=True)
                elif kind == "ck":
                    pe.wait_ge(cw_in, 32)
                    pe.wait_ge(c_in[b], 16)
                    last = mm(g[:, 0:L], cwkT[:, :], cT_sb[:, b, :], start=True, stop=True)
                else:
                    for q in range(LT):
                        last = mm(g[:, q * D:(q + 1) * D], cT_sb[:, b, q * P:(q + 1) * P], cwvT[:, :],
                                  start=True, stop=True)
                last.then_inc(g_ready, 1)

            def place(h):
                return h // PAIRS, (h % PAIRS) // 2

            def cross_scores(b, u):
                lt, j = u // PAIRS, u % PAIRS
                n = b * UNITS + u
                if u == 0:
                    pe.wait_ge(ck_in[b % 2], 16 * K_READS * (b // 2 + 1))
                    pe.wait_ge(cq_in[b % 2], 16 * Q_READS * (b // 2 + 1))
                if n >= BANKS:
                    pe.wait_ge(cE_done, n - BANKS + 1)
                mm(cS[n % BANKS][:, :], cK[:, b % 2, j, lt * P:(lt + 1) * P],
                   cQ[:, b % 2, j:j + PAIRS + 1:PAIRS, :], start=True, stop=True).then_inc(cs_ready, 1)

            def cross_pv(b, lt, i):
                n = b * LT + lt
                if i == 0:
                    pe.wait_ge(cV_done, 2 * (n + 1))
                    if lt == 0 and b >= 1:
                        pe.wait_ge(o_out, b)
                first = PAIRS * (i // 4) + 4 * (i % 2) + i % 4 // 2
                for h in (first, first + 2):
                    r, c = place(h)
                    last = mm(oC[TILE_COLS * c:TILE_COLS * (c + 1), r * S:(r + 1) * S],
                              cV[:, n % 2, h, :], cE[:, n % 2, h, :],
                              start=(lt == 0 and r == 0 and h % 2 == 0),
                              stop=(lt == LT - 1 and r == 1 and h % 2 == 1), skip_group_check=True)
                if i == PAIRS - 1:
                    last.then_inc(c_pv, 1)

            def norm_step(a, k, b):
                kind = "NC"[a] + k
                if k == "2":
                    g = begin(kind, b)
                    pe.wait_ge(o_out, b + 1)
                    for q in range(QT):
                        for r in range(2):
                            last = nc.tensor.transpose(g[:, (q * 2 + r) * P:(q * 2 + r + 1) * P],
                                                       oSb[:, r * S + q * P:r * S + (q + 1) * P], ident[:, :])
                elif k == "4":
                    g = begin(kind, b)
                    if a == 0:
                        pe.wait_ge(a_in, 16 * (b + 1))
                    else:
                        pe.wait_ge(a_done, b + 1)
                    for q in range(QT):
                        last = nc.tensor.transpose(g[:, q * P:(q + 1) * P], aN[:, a, q, :], ident[:, :])
                elif k == "5":
                    g = begin(kind, b)
                    pe.wait_ge(w_in, 16 * 4)
                    pe.wait_ge(at_done[a], b + 1)
                    for q in range(QT):
                        last = mm(g[:, q * D:(q + 1) * D], aT[:, a, q * P:(q + 1) * P],
                                  (woT, cwoT)[a][:, :], start=True, stop=True)
                elif k == "9":
                    g = begin(kind, b)
                    pe.wait_ge(ln_done[a], QT * (b + 1))
                    for q in range(QT):
                        src = x1[:, b, q, :] if a == 0 else x2[:, b * QT + q, 0:D]
                        last = nc.tensor.transpose(g[:, q * P:(q + 1) * P], src, ident[:, :])
                elif a == 0:
                    g = begin(kind, b)
                    pe.wait_ge(xt_done[0], b + 1)
                    last = mm(g[:, 0:S], cwqT[:, :], x1T[:, :], start=True, stop=True)
                else:
                    g = begin(kind, b)
                    pe.wait_ge(xt_done[1], b + 1)
                    for q in range(QT):
                        last = mm(g[:, q * E:(q + 1) * E], x2T[:, q * P:(q + 1) * P], wg[:, :],
                                  start=True, stop=True)
                last.then_inc(g_ready, 1)

            def ranks(b):
                g = begin("R", b)
                pe.wait_ge(route, b + 1)
                ts, m = slice(QT * b, QT * (b + 1)), QT * E

                def sums(at, *terms):
                    for i, (a, o) in enumerate(terms):
                        ins = mm(g[:, at:at + (m if at < 3 * m else E)], a[:, :], o, start=(i == 0),
                                 stop=(i == len(terms) - 1), skip_group_check=True)
                    return ins

                so_far = before[:, 0, QT * (b + 1):QT * (b + 1) + 1, :]
                alone = ((lower, hotb[:, 1, ts, :]), (ones, before[:, 1, ts, :]))
                sums(0, (lower, hotb[:, 0, ts, :]), (ones, before[:, 0, ts, :]))
                sums(m, *alone, (ones, so_far.to_broadcast([P, QT, E])))
                sums(2 * m, *alone)
                sums(3 * m, (ones, before[:, 0, QT * (b + 1), :])).then_inc(g_ready, 1)

            def work(row):
                for k, b, n in row:
                    if k in ("A", "ck", "cv"):
                        project(k, b, n)
                    elif k == "R":
                        ranks(b)
                    elif k[0] in "NC" and k != "C1":
                        norm_step("NC".index(k[0]), k[1:], b)

            pe.wait_ge(cchain, 2)
            work(prologue)
            for i in range(B):
                for s in range(UNITS):
                    if i == 0 and s == 0:
                        for a in range(AHEAD):
                            cross_scores(0, a)
                    n = i * UNITS + s + AHEAD
                    if n < B * UNITS:
                        cross_scores(n // UNITS, n % UNITS)
                    n = i * LT + s // PAIRS - 1
                    if n >= 0 and s % PAIRS in PV_AT:
                        for k in range(2):
                            cross_pv(n // LT, n % LT, 2 * PV_AT.index(s % PAIRS) + k)
                    work(rows_at(i * UNITS + s, LEAD_PE))
            for k in range(PAIRS):
                cross_pv(B - 1, LT - 1, k)
            work(last_norm)

            pe.wait_ge(cE_done, B * UNITS)

            def rows_transposed(e):
                p_, s = e // 2, e % 2
                pe.wait_ge(xs_in[p_], 48)
                if e >= 2:
                    pe.wait_ge(xt_cp, e - 1)
                for c, col in ((0, 2 * s), (1, 2 * s + 1), (2, 4))[0:3 - s]:
                    last = nc.tensor.transpose(cS[s][:, c * P:(c + 1) * P], xs[:, p_, col, 0:D], ident[:, :])
                last.then_inc(xt_mm, 1)

            def up(e):
                pe.wait_ge(xt_cp, e + 1)
                for f in range(FT):
                    n = e * FT + f
                    if n >= 4:
                        pe.wait_ge(gelu, n - 3)
                    mm(h_banks[n % 4][:, 0:CAP], fc[:, e, f * P:(f + 1) * P],
                       xsT[:, e * CAP:(e + 1) * CAP], start=True, stop=True).then_inc(h_mm, 1)

            def down(e):
                s = e % 2
                pe.wait_ge(gelu, FT * (e + 1))
                for c in range(2 + s):
                    n = y_tiles(e) - (2 + s) + c
                    y = y_banks[n % 2]
                    if n >= 2:
                        pe.wait_ge(y_cp, n - 1)
                    for f in range(FT):
                        start_stop = dict(start=(f == 0), stop=(f == FT - 1), skip_group_check=True)
                        if c < 2:
                            at = s * REST + c * P
                            last = mm(y[:, 0:D], hT[:, e % 3, f, at:at + P], pj[:, e, f, :], **start_stop)
                        else:
                            mm(y[0:REST, 0:D], hT[:, (e - 1) % 3, f, MAIN:CAP], pj[:, e - 1, f, :], **start_stop)
                            last = mm(y[REST:2 * REST, 0:D], hT[:, e % 3, f, 0:REST], pj[:, e, f, :], **start_stop)
                    last.then_inc(y_mm, 1)

            pe.wait_ge(moe_in, 16 * 2 * E)
            pe.wait_ge(rank_read, B)
            pe.wait_ge(scat[B - 1], 16 * TOPK * QT)
            for _ in range(WARM):
                mm(cS[2][:, 0:D], ident[:, :], ident[:, :], start=True, stop=True)
            rows_transposed(0)
            rows_transposed(1)
            up(0)
            for e in range(E):
                if e + 2 < E:
                    rows_transposed(e + 2)
                if e + 1 < E:
                    up(e + 1)
                down(e)

        @block.scalar
        def _(act):
            A = nc.scalar.activation

            def copy_proj(kind, b, use):
                n = split_no(kind, b)
                if n >= 2:
                    act.wait_ge(split, 4 * (n - 1))
                await_use(act, *use)
                scale = CROSS_SCALE if kind == "cq" else 1.0
                m = split_len(kind)
                ins = A(proj[:, n % 2, 0:m], bank(*use)[:, 0:m], ACT.Copy, scale=scale)
                ins.then_inc(proj_out, 1)

            def work(row):
                for k, b, n in row:
                    if k == "ck":
                        copy_proj("ck", b, (k, b, 0))
                    elif k == "N10":
                        copy_proj("cq", b, (k, b, 0))
                    elif k in COPIES_BY_ACT:
                        copy_out(act, k, b)
                    elif k == "A":
                        await_use(act, k, b, n)
                        m = b * QT + n
                        if m >= RING:
                            for h in range(2):
                                act.wait_ge(pv_done[m % 2][h], (m - RING) // 2 + 1)
                        A(qkv[:, m % RING, :], bank(k, b, n)[:, 0:3 * D], ACT.Copy).then_inc(qkv_out, 1)
                    elif k == "p":
                        m = b * QT + n
                        act.wait_ge(s_ready, m + 1)
                        if m >= 2:
                            act.wait_ge(o_done, m - 1)
                        A(sP[:, m % 2, :], sS[:, m % 2, :], ACT.Exp, scale=SELF_SCALE).then_inc(p_done, 1)

            work(prologue)
            for i in range(B):
                for s in range(UNITS):
                    n = i * UNITS + s
                    lt, j = s // PAIRS, s % PAIRS
                    g = i * LT + lt
                    act.wait_ge(cm_done, n + 1)
                    if j == 0 and g >= 2:
                        act.wait_ge(c_pv, g - 1)
                        act.wait_ge(crec_done, g - 1)
                    for hf in range(2):
                        ins = A(cE[:, g % 2, hf * PAIRS + j, :], cS[n % BANKS][:, hf * S:(hf + 1) * S], ACT.Exp,
                                bias=cmx[:, g % 2, hf, j:j + 1],
                                accum_out=csum[:, g % 2, hf * PAIRS + j:hf * PAIRS + j + 1])
                    ins.then_inc(cE_done, 1)
                    work(rows_at(i * UNITS + s))
            work(last_norm)
            act.wait_ge(dz_done, 1)
            A(ez[:, :], dz[:, :], ACT.Exp).then_inc(ex_done, 1)
            for n in range(E * FT):
                e, f = n // FT, n % FT
                act.wait_ge(h_mm, n + 1)
                if e >= 3:
                    act.wait_ge(y_mm, y_tiles((e - 3) | 1))
                A(hT[:, e % 3, f, :], h_banks[n % 4][:, 0:CAP], ACT.Gelu).then_inc(gelu, 1)
            act.wait_ge(w_done, 1)
            for g in range(GROUPS):
                act.wait_ge(gath[g], 16 * TOPK)
                for t in range(g * GT, (g + 1) * GT):
                    ins = A(yg[:, t, :], yg[:, t, :], ACT.Identity, scale=w[:, 0, t:t + 1])
                ins.then_inc(f_weighed, 1)
            for g in range(GROUPS):
                act.wait_ge(f_shift, g + 1)
                for t in range(g * GT, (g + 1) * GT):
                    ins = A(fin[:, t, :], res[:, t, :], ACT.Identity, scale=frstd[:, t:t + 1],
                            bias=fshift[:, t:t + 1])
                ins.then_inc(f_ln, 1)

        @block.vector
        def _(dve):
            V = nc.vector
            V.memset(zero[:, :], 0.0).then_inc(zeroed, 1)
            V.memset(cV[:, :, :, :], 0.0).then_inc(pads, 1)
            V.memset(zrow[:, :], 0.0).then_inc(zeroed, 1)
            V.memset(vOne[:, :, :, :, :], 1.0).then_inc(pads, 1)

            steps_done = [0]

            def after(ins):
                steps_done[0] += 1
                ins.then_inc(s_step, 1)
                dve.wait_ge(s_step, steps_done[0])

            def self_step(k, b, q, h):
                n = b * QT + q
                m = n % 2
                S_ = sS[:, m, :].rearrange("p (a k) -> p a k", a=HEADS)
                if k == "s":
                    dve.wait_ge(qk_done[m], 2 * (n // 2) + h + 1)
                    W = HEADS * HEADS // 2
                    V.tensor_reduce(out=sS[:, m, h * W:(h + 1) * W],
                                    in_=prod[:, m, h * W * HD:(h + 1) * W * HD].rearrange("p (s d) -> p s d", d=HD),
                                    axis=AX.X, op=ALU.add).then_inc(s_sum, 1)
                elif k == "mx":
                    dve.wait_ge(s_sum, 2 * (n + 1))
                    after(V.tensor_reduce(out=smx[:, m, :], in_=S_, axis=AX.X, op=ALU.max))
                    V.tensor_tensor(out=S_, in0=S_, in1=smx[:, m, :].unsqueeze(2).to_broadcast([P, HEADS, HEADS]),
                                    op=ALU.subtract).then_inc(s_ready, 1)
                elif k == "sm":
                    dve.wait_ge(p_done, n + 1)
                    after(V.tensor_reduce(out=ssum[:, m, :], in_=sP[:, m, :].rearrange("p (a k) -> p a k", a=HEADS),
                                          axis=AX.X, op=ALU.add))
                    V.reciprocal(srec[:, m, :], ssum[:, m, :]).then_inc(srec_done, 1)
                elif k == "o":
                    dve.wait_ge(pv_done[m][h], n // 2 + 1)
                    W = HEADS * HD // 2
                    V.tensor_reduce(out=sOn[:, m, h * W:(h + 1) * W],
                                    in_=prod[:, m, h * W * HEADS:(h + 1) * W * HEADS]
                                    .rearrange("p (s k) -> p s k", k=HEADS), axis=AX.X, op=ALU.add).then_inc(o_sum, 1)
                    if h == 1:
                        dve.wait_ge(srec_done, n + 1)
                        dve.wait_ge(o_sum, 2 * (n + 1))
                        if n >= 2:
                            dve.wait_ge(a_st[q], 16 * b)
                        V.tensor_tensor(out=sO[:, m, :].rearrange("p (a d) -> p a d", d=HD),
                                        in0=sOn[:, m, :].rearrange("p (a d) -> p a d", d=HD),
                                        in1=srec[:, m, :].unsqueeze(2).to_broadcast([P, HEADS, HD]), op=ALU.mult
                                        ).then_inc(o_done, 1)

            count = [0]

            def link(ins):
                count[0] += 1
                ins.then_inc(chain, 1)
                dve.wait_ge(chain, count[0])

            def choose(b):
                tiles = range(QT * b, QT * (b + 1))
                dve.wait_ge(log_done, b + 1)
                for t in tiles:
                    ins = V.max(top[:, t, :], logits[:, t, :])
                link(ins)
                for t in tiles:
                    ins = V.max_index(topi[:, t, :], top[:, t, :], logits[:, t, :])
                link(ins)
                ts = slice(QT * b, QT * (b + 1))
                link(V.tensor_copy(ef[:, :, ts], topi[:, ts, 0:TOPK].rearrange("p t k -> p k t")))
                if b == 0:
                    dve.wait_ge(consts, 2)
                    link(V.memset(before[:, :, 0, :], 0.0))
                for k in range(TOPK):
                    ins = V.tensor_tensor(out=hotb[:, k, ts, :], in0=ef[:, k, ts].unsqueeze(2).to_broadcast([P, QT, E]),
                                          in1=iotaE[:, :].unsqueeze(1).to_broadcast([P, QT, E]), op=ALU.is_equal)
                link(ins)
                for t in tiles:
                    ins = V.tensor_tensor(out=before[:, :, t + 1, :], in0=before[:, :, t, :], in1=hotb[:, :, t, :],
                                          op=ALU.add)
                    if t < tiles[-1]:
                        link(ins)
                ins.then_inc(route, 1)
                for k in range(TOPK):
                    ins = V.tensor_scalar(base_of[:, k, ts], ef[:, k, ts], float(CAP), float(k * (CAP - 1)),
                                          ALU.mult, ALU.add)
                link(ins)

            def slots(b):
                ts, m = slice(QT * b, QT * (b + 1)), QT * E
                await_use(dve, "R", b)
                g = bank("R", b)
                V.tensor_tensor(out=rank[:, 0:2, :, :], in0=g[:, 0:2 * m].rearrange("p (k t e) -> p k t e", k=2, e=E),
                                in1=hotb[:, :, ts, :], op=ALU.mult)
                if b == B - 1:
                    V.tensor_copy(firsts[:, :], g[:, 3 * m:3 * m + E])
                V.scalar_tensor_tensor(out=rank[:, 2, :, :].rearrange("p t e -> p (t e)"), in0=g[:, 2 * m:3 * m],
                                       scalar=-1.0, in1=hotb[:, 1, ts, :].rearrange("p t e -> p (t e)"),
                                       op0=ALU.mult, op1=ALU.mult).then_inc(rank_read, 1)
                dve.wait_ge(rank_read, b + 1)
                link(V.tensor_reduce(out=place_of[:, ts, :].rearrange("p t k -> p k t"), in_=rank[:, :, :, :],
                                     axis=AX.X, op=ALU.add))
                V.tensor_scalar(over[:, :, :], place_of[:, ts, 0:2].rearrange("p t k -> p k t"), float(CAP),
                                2.0 * SLOTS, ALU.is_ge, ALU.mult)
                link(V.tensor_tensor(out=slotf[:, :, :], in0=place_of[:, ts, 0:3:2].rearrange("p t k -> p k t"),
                                     in1=base_of[:, :, ts], op=ALU.add))
                V.tensor_tensor(out=slot[:, :, ts], in0=slotf[:, :, :], in1=over[:, :, :], op=ALU.add
                                ).then_inc(slot_done, 1)

            def sums(g):
                dve.wait_ge(cE_done, PAIRS * (g + 1))
                if g >= 2:
                    dve.wait_ge(cV_done, 2 * (g - 1))
                V.reciprocal(crec[:, g % 2, :], csum[:, g % 2, :]).then_inc(crec_done, 1)

            def norm_step(a, k, b):
                kind = "NC"[a] + k
                await_use(dve, kind, b)
                g = bank(kind, b)
                if k == "2":
                    t = g[:, :].rearrange("p (c x) -> p c x", x=TILE_COLS)[:, :, 0:2 * CV] \
                        .rearrange("p c (s d) -> p c s d", s=2)
                    r = oRec[:, :].rearrange("p (c s) -> p c s", s=2)
                    V.reciprocal(r, t[:, :, :, HD]).then_inc(rec_done, 1)
                    dve.wait_ge(rec_done, b + 1)
                    ins = V.tensor_tensor(
                        out=aN[:, a].rearrange("p q (c s d) -> p (q c) s d", s=2, d=HD), in0=t[:, :, :, 0:HD],
                        in1=r.unsqueeze(3).to_broadcast([P, HEADS, 2, HD]), op=ALU.mult)
                    ins.then_inc(a_done, 1)
                else:
                    if a == 0:
                        dve.wait_ge(bias_added, b + 1)
                    src = x_sb[:, b] if a == 0 else x1[:, b]
                    ins = V.tensor_tensor(out=pre[:, a].rearrange("p q d -> p (q d)"), in0=g[:, 0:QT * D],
                                          in1=src.rearrange("p q d -> p (q d)"), op=ALU.add)
                    ins.then_inc(pre_done[a], 1)

            def layer_norm(a, b):
                dve.wait_ge(pre_done[a], b + 1)
                for q in range(QT):
                    V.bn_stats(stats[:, a, q, :], pre[:, a, q, :]).then_inc(st_done[a], 1)
                for q in range(QT):
                    dve.wait_ge(st_done[a], QT * b + q + 1)
                    V.bn_aggr(mv[:, a, q, :], stats[:, a, q, :]).then_inc(mv_done[a], 1)
                dve.wait_ge(mv_done[a], QT * (b + 1))
                V.tensor_scalar(vare[:, a, :], mv[:, a, :, 1], EPS, None, ALU.add).then_inc(vare_done[a], 1)

            def normalise(a, b):
                dve.wait_ge(rstd_done[a], b + 1)
                for q in range(QT):
                    dst = x1[:, b, q, :] if a == 0 else x2[:, b * QT + q, 0:D]
                    V.tensor_scalar(dst, pre[:, a, q, :], mv[:, a, q, 0:1], rstd[:, a, q:q + 1],
                                    ALU.subtract, ALU.mult).then_inc(ln_done[a], 1)

            def work(row):
                for k, b, n in row:
                    if k == "R":
                        choose(b)
                        slots(b)
                    elif k in ("qk", "pv"):
                        product(dve, V, k, b, n)
                    elif k in ("mx", "sm"):
                        self_step(k, b, n, 0)
                    elif k in ("s", "o"):
                        self_step(k, b, n // 2, n % 2)
                    elif k in ("cv", "C1", "N4", "C4", "N9", "C9", "C10"):
                        if k[1:] == "9":
                            normalise("NC".index(k[0]), b)
                        copy_out(dve, k, b)
                    elif k in ("C2", "N5", "C5"):
                        norm_step("NC".index(k[0]), k[1:], b)
                        if k[1:] == "5":
                            layer_norm("NC".index(k[0]), b)

            work(prologue)
            for i in range(B):
                for s in range(UNITS):
                    n = i * UNITS + s
                    lt, j = s // PAIRS, s % PAIRS
                    g = i * LT + lt
                    dve.wait_ge(cs_ready, n + 1)
                    if g >= 2 and j == 0:
                        dve.wait_ge(cE_done, PAIRS * (g - 1))
                    V.tensor_reduce(out=cmx[:, g % 2, :, j], in_=cS[n % BANKS][:, :].rearrange("p (a t) -> p a t", a=2),
                                    axis=AX.X, op=ALU.max, negate=True).then_inc(cm_done, 1)
                    if s % PAIRS == 1 and g >= 1:
                        sums(g - 1)
                    work(rows_at(i * UNITS + s))
            sums(B * LT - 1)
            work(last_norm)

            V.tensor_tensor(out=dz[:, :], in0=top[:, :, 1], in1=top[:, :, 0], op=ALU.subtract).then_inc(dz_done, 1)
            V.tensor_scalar(keep[:, 0, :], place_of[:, :, 0], float(CAP), None, ALU.is_lt)
            link(V.tensor_tensor(out=queue[:, :, :], in0=hotb[:, 1, :, :],
                                 in1=firsts[:, :].unsqueeze(1).to_broadcast([P, TT, E]), op=ALU.mult))
            link(V.tensor_reduce(out=behind[:, :], in_=queue[:, :, :], axis=AX.X, op=ALU.add))
            link(V.tensor_tensor(out=behind[:, :], in0=behind[:, :], in1=place_of[:, :, 2], op=ALU.subtract))
            V.tensor_scalar(keep[:, 1, :], behind[:, :], float(CAP), None, ALU.is_lt)
            dve.wait_ge(ex_done, 1)
            link(V.tensor_scalar(ez1[:, :], ez[:, :], 1.0, None, ALU.add))
            link(V.reciprocal(w[:, 0, :], ez1[:, :]))
            link(V.tensor_tensor(out=w[:, 1, :], in0=w[:, 0, :], in1=ez[:, :], op=ALU.mult))
            V.tensor_tensor(out=w[:, :, :], in0=w[:, :, :], in1=keep[:, :, :], op=ALU.mult).then_inc(w_done, 1)
            dve.wait_ge(w_done, 1)
            V.tensor_tensor(out=second[:, :, 0:4].rearrange("p e (s c) -> p e s c", s=2),
                            in0=iotaS[:, 0:2].unsqueeze(1).unsqueeze(1).to_broadcast([P, E // 2, 2, 2]),
                            in1=firsts[:, :].rearrange("p (e s) -> p e s", s=2).unsqueeze(3)
                            .to_broadcast([P, E // 2, 2, 2]), op=ALU.is_ge)
            link(V.tensor_scalar(iotaS[REST:P, 2:3], iotaS[REST:P, 2:3], -float(REST), None, ALU.add))
            for s in range(2):
                half_ = slice(s * REST, (s + 1) * REST)
                ins = V.tensor_tensor(out=second[half_, :, 4], in0=iotaS[half_, 2:3].to_broadcast([REST, E // 2]),
                                      in1=firsts[half_, s:E:2], op=ALU.is_ge)
            link(ins)
            link(V.tensor_scalar(second[:, :, :], second[:, :, :], float(T), float(NONE), ALU.mult, ALU.add))
            def copy_rows(e):
                dve.wait_ge(xt_mm, e + 1)
                if e % 2 == 0:
                    ins = V.tensor_copy(xsT[:, e * CAP:(e + 1) * CAP + REST], cS[0][:, 0:CAP + REST])
                else:
                    ins = V.tensor_copy(xsT[:, e * CAP + REST:(e + 1) * CAP], cS[1][:, 0:MAIN])
                ins.then_inc(xt_cp, 1)

            copy_rows(0)
            copy_rows(1)
            for e in range(E):
                if e + 2 < E:
                    copy_rows(e + 2)
                if e == 0:
                    for pair in range(E // 2):
                        dve.wait_ge(xs_in[pair], 48)
                    V.tensor_tensor(out=row_of[:, :, :], in0=xs[:, :, :, D], in1=second[:, :, :], op=ALU.add
                                    ).then_inc(rows_done, 1)
                s = e % 2
                for c in range(2 + s):
                    n = y_tiles(e) - (2 + s) + c
                    dve.wait_ge(y_mm, n + 1)
                    if e >= 2 and c == 0:
                        dve.wait_ge(ys_out[s], 16 * (2 + s) * (e // 2))
                    V.tensor_copy(ys[:, s, c, :], y_banks[n % 2][:, 0:D]).then_inc(y_cp, 1)
            fc_n = [0]

            def flink(ins):
                fc_n[0] += 1
                ins.then_inc(f_chain, 1)
                dve.wait_ge(f_chain, fc_n[0])

            for g in range(GROUPS):
                tiles = range(g * GT, (g + 1) * GT)
                ts = slice(g * GT, (g + 1) * GT)
                dve.wait_ge(gath[g], 16 * TOPK)
                dve.wait_ge(f_first, g + 1)
                for t in tiles:
                    ins = V.scalar_tensor_tensor(out=res[:, t, :], in0=yg[:, TT + t, :], scalar=w[:, 1, t:t + 1],
                                                 in1=res[:, t, :], op0=ALU.mult, op1=ALU.add)
                flink(ins)
                for t in tiles:
                    ins = V.bn_stats(fstats[:, t, :], res[:, t, :])
                flink(ins)
                for t in tiles:
                    ins = V.bn_aggr(fmv[:, t, :], fstats[:, t, :])
                flink(ins)
                V.tensor_scalar(fneg[:, ts], fmv[:, ts, 0], -1.0, None, ALU.mult)
                V.tensor_scalar(fvare[:, ts], fmv[:, ts, 1], EPS, None, ALU.add).then_inc(f_vare, 1)


def kernel(x, ctx_1024, L0_attn_Wq, L0_attn_Wk, L0_attn_Wv, L0_attn_Wo, L0_attn_bo,
           L0_xattn_Wq, L0_xattn_Wk, L0_xattn_Wv, L0_xattn_Wo, L0_ffn_w_g, L0_ffn_c_fc, L0_ffn_c_proj):
    import numpy as np
    import concourse.bacc as bacc
    from concourse.bass_utils import run_bass_kernel_spmd

    def columns_by_feature(w):
        d = w.shape[1]
        return w.T.reshape(d, 2, PAIRS, d // HEADS).transpose(0, 1, 3, 2).reshape(d, d)

    a = np.asarray
    arrays = {
        "xT": a(x).transpose(2, 0, 1), "x": a(x), "ctxT": a(ctx_1024).transpose(2, 0, 1),
        "attn_wqT": a(L0_attn_Wq).T, "attn_wkT": a(L0_attn_Wk).T,
        "attn_wvT": a(L0_attn_Wv).T, "attn_woT": a(L0_attn_Wo).T, "attn_bo": a(L0_attn_bo),
        "x_wqT": columns_by_feature(a(L0_xattn_Wq)), "x_wkT": columns_by_feature(a(L0_xattn_Wk)),
        "x_wvT": a(L0_xattn_Wv).T, "x_woT": a(L0_xattn_Wo).T,
        "w_g": a(L0_ffn_w_g), "c_fc": a(L0_ffn_c_fc), "c_proj": a(L0_ffn_c_proj),
    }
    arrays = {k: np.ascontiguousarray(v) for k, v in arrays.items()}
    nc = bacc.Bacc("TRN2", target_bir_lowering=False, num_devices=1)
    args = [nc.dram_tensor(k, v.shape, mybir.dt.from_np(v.dtype), kind="ExternalInput").ap()
            for k, v in arrays.items()]
    out = nc.dram_tensor("out", a(x).shape, F32, kind="ExternalOutput").ap()
    decoder_layer(nc, *args, out)
    r = run_bass_kernel_spmd(nc, [arrays], core_ids=[0])
    return r.results[0]["out"]
```
